# Optimizing a Trainium2 kernel written in Bass

```python
import numpy as np
import jax
import jax.numpy as jnp

def _softmax(x, axis=-1):
    return jax.nn.softmax(x, axis=axis)

def _gelu(x):
    return jax.nn.gelu(x, approximate=True)

def _silu(x):
    return jax.nn.silu(x)

def _sigmoid(x):
    return jax.nn.sigmoid(x)

def _layernorm(x, axis=-1, eps=1e-05):
    m = jnp.mean(x, axis=axis, keepdims=True)
    v = jnp.var(x, axis=axis, keepdims=True)
    return (x - m) / jnp.sqrt(v + eps)

def _scatter_add(tgt, idx, src, axis=0):
    return tgt.at[idx].add(src)

def _segment_sum(src, seg, n):
    return jax.ops.segment_sum(src, seg, n)
kernel_name = 'mk_xattn_ffn_d1_seqx_r8_eb546c'

def setup_inputs(seed: int=0):
    np.random.seed(seed)
    _w = jnp.asarray

    def _rec_inputs():
        import jax
        import jax.numpy as jnp
        _rk = jax.random.key(seed)
        x = 7.22e-05 + 1 * jax.random.normal(jax.random.fold_in(_rk, 1), (4, 512, 128), jnp.float32)
        _lenS = 512 - jax.random.randint(jax.random.fold_in(_rk, 7), (4,), 0, max(1, 512 // 4) + 1, jnp.int32)
        _lenS2 = 77 - jax.random.randint(jax.random.fold_in(_rk, 8), (4,), 0, max(1, 77 // 4) + 1, jnp.int32)
        _ctx_1024P = jax.random.normal(jax.random.fold_in(_rk, 11), (4, 16, 128), jnp.float32)
        _ctx_1024c = jax.random.dirichlet(jax.random.fold_in(_rk, 511), 0.3 * jnp.ones((16,), jnp.float32), (4, 77))
        _ctx_1024t = jnp.einsum('bsk,bkd->bsd', _ctx_1024c, _ctx_1024P)
        _ctx_1024t = _ctx_1024t * jax.lax.rsqrt(jnp.mean(jnp.square(_ctx_1024t)) + 1e-12) * 0.953939
        ctx_1024 = 4.13588e-05 + 0.999923 * (_ctx_1024t + 0.3 * jax.random.normal(jax.random.fold_in(_rk, 611), (4, 77, 128), jnp.float32))
        _validS = jnp.arange(512)[None, :] < _lenS[:, None]
        _validS2 = jnp.arange(77)[None, :] < _lenS2[:, None]
        _causal = jnp.tril(jnp.ones((512, 512), dtype=bool))
        mask_BxS2_bk0 = jnp.logical_not(jnp.broadcast_to(_validS2[:, :], (4, 77)))
        return (x, ctx_1024, mask_BxS2_bk0)
    x, ctx_1024, mask_BxS2_bk0 = _rec_inputs()

    def _L0_xattn_setup():
        import jax, jax.numpy as jnp
        import numpy as np
        B, S, D, H = (4, 256, 128, 16)
        DH = D // H
        key = jax.random.key(seed)
        ks = jax.random.split(key, 12)
        scale = 1.0 / np.sqrt(D)
        inp = {'query': jax.random.normal(ks[0], (B, S, D), jnp.float32), 'key': jax.random.normal(ks[1], (B, S, D), jnp.float32), 'value': jax.random.normal(ks[2], (B, S, D), jnp.float32), 'key_padding_mask': jax.random.randint(ks[3], (B, S), 0, 2).astype(bool), 'Wq': jax.random.normal(ks[4], (D, H * DH), jnp.float32) * scale, 'bq': jnp.zeros((H * DH,), jnp.float32), 'Wk': jax.random.normal(ks[5], (D, H * DH), jnp.float32) * scale, 'bk': jnp.zeros((H * DH,), jnp.float32), 'Wv': jax.random.normal(ks[6], (D, H * DH), jnp.float32) * scale, 'bv': jnp.zeros((H * DH,), jnp.float32), 'Wo': jax.random.normal(ks[7], (H * DH, D), jnp.float32) * scale, 'bo': jnp.zeros((D,), jnp.float32)}
        return inp
    _L0_xattn_all = _L0_xattn_setup()
    _L0_xattn_in = {k: v for k, v in _L0_xattn_all.items() if k in ('Wq', 'bq', 'Wk', 'bk', 'Wv', 'bv', 'Wo', 'bo')}
    del _L0_xattn_all

    def _L0_ffn_setup():
        import jax, jax.numpy as jnp
        import numpy as np
        TOP_K = 2
        key = jax.random.key(seed)
        ks = jax.random.split(key, 5)
        B, T, D, F, E = (2, 256, 128, 512, 8)
        x = jax.random.normal(ks[0], (B, T, D), dtype=jnp.float32)
        router_w = jax.random.normal(ks[1], (D, E + 1), dtype=jnp.float32) * 0.02
        router_b = jax.random.normal(ks[2], (E + 1,), dtype=jnp.float32) * 0.02
        w1 = jax.random.normal(ks[3], (E, D, F), dtype=jnp.float32) * 0.02
        w2 = jax.random.normal(ks[4], (E, F, D), dtype=jnp.float32) * 0.02
        return {'x': x, 'router_w': router_w, 'router_b': router_b, 'w1': w1, 'w2': w2}
    _L0_ffn_all = _L0_ffn_setup()
    _L0_ffn_in = {k: v for k, v in _L0_ffn_all.items() if k in ('router_w', 'router_b', 'w1', 'w2')}
    del _L0_ffn_all
    return {'x': x, 'ctx_1024': ctx_1024, 'mask_BxS2_bk0': mask_BxS2_bk0, 'L0_xattn_Wq': _L0_xattn_in['Wq'], 'L0_xattn_bq': _L0_xattn_in['bq'], 'L0_xattn_Wk': _L0_xattn_in['Wk'], 'L0_xattn_bk': _L0_xattn_in['bk'], 'L0_xattn_Wv': _L0_xattn_in['Wv'], 'L0_xattn_bv': _L0_xattn_in['bv'], 'L0_xattn_Wo': _L0_xattn_in['Wo'], 'L0_xattn_bo': _L0_xattn_in['bo'], 'L0_ffn_router_w': _L0_ffn_in['router_w'], 'L0_ffn_router_b': _L0_ffn_in['router_b'], 'L0_ffn_w1': _L0_ffn_in['w1'], 'L0_ffn_w2': _L0_ffn_in['w2']}

def reference(x, ctx_1024, mask_BxS2_bk0, L0_xattn_Wq, L0_xattn_bq, L0_xattn_Wk, L0_xattn_bk, L0_xattn_Wv, L0_xattn_bv, L0_xattn_Wo, L0_xattn_bo, L0_ffn_router_w, L0_ffn_router_b, L0_ffn_w1, L0_ffn_w2):
    import jax
    import jax.numpy as jnp

    def _L0_xattn_ref(query, key, value, key_padding_mask, Wq, bq, Wk, bk, Wv, bv, Wo, bo):
        import jax, jax.numpy as jnp
        import numpy as np
        B, S, D, H = (4, 256, 128, 16)
        DH = D // H
        b, nq, _ = query.shape
        nk = key.shape[-2]
        q = (query @ Wq + bq).reshape(b, nq, H, DH).transpose(0, 2, 1, 3)
        k = (key @ Wk + bk).reshape(b, nk, H, DH).transpose(0, 2, 1, 3)
        v = (value @ Wv + bv).reshape(b, nk, H, DH).transpose(0, 2, 1, 3)
        scores = jnp.einsum('bhqd,bhkd->bhqk', q, k) / np.sqrt(DH)
        mask = key_padding_mask[:, None, None, :]
        scores = jnp.where(mask, -jnp.inf, scores)
        w = jax.nn.softmax(scores, axis=-1)
        attn = jnp.einsum('bhqk,bhkd->bhqd', w, v)
        attn = attn.transpose(0, 2, 1, 3).reshape(b, nq, H * DH)
        return attn @ Wo + bo

    def _L0_ffn_ref(x, router_w, router_b, w1, w2):
        import jax, jax.numpy as jnp
        import numpy as np
        TOP_K = 2
        E = w1.shape[0]
        logits = x @ router_w + router_b
        probs = jax.nn.softmax(logits, axis=-1)
        top_v, top_i = jax.lax.top_k(probs, TOP_K)
        gates = jnp.sum(jax.nn.one_hot(top_i, E + 1, dtype=x.dtype) * top_v[..., None], axis=-2)
        h = jax.nn.gelu(jnp.einsum('btd,edf->ebtf', x, w1), approximate=False)
        y = jnp.einsum('ebtf,efd->ebtd', h, w2)
        out = jnp.einsum('bte,ebtd->btd', gates[..., :E], y) + gates[..., E:] * x
        return out
    x = x + _L0_xattn_ref(_layernorm(x, axis=-1), ctx_1024, ctx_1024, mask_BxS2_bk0, L0_xattn_Wq, L0_xattn_bq, L0_xattn_Wk, L0_xattn_bk, L0_xattn_Wv, L0_xattn_bv, L0_xattn_Wo, L0_xattn_bo)
    x = x + _L0_ffn_ref(_layernorm(x, axis=-1), L0_ffn_router_w, L0_ffn_router_b, L0_ffn_w1, L0_ffn_w2)
    return x

_drawn_inputs = setup_inputs


def setup_inputs(seed=0):
    import zlib

    import numpy as np

    out = dict(_drawn_inputs(seed))
    spreads = {'L0_xattn_bq': (0.0, 0.325),
     'L0_xattn_bk': (0.0, 0.8),
     'L0_xattn_bv': (0.0, 0.1),
     'L0_xattn_bo': (0.0, 0.1)}
    factors = {'L0_ffn_router_b': 4.743, 'L0_ffn_w1': 6.631, 'L0_ffn_w2': 6.495}
    for name, (base, spread) in spreads.items():
        noise = np.random.default_rng([zlib.crc32(name.encode()), seed]).standard_normal(out[name].shape)
        drawn = base * np.exp(spread * noise) if base else spread * noise
        out[name] = jnp.asarray(drawn.astype(out[name].dtype))
    for name, factor in factors.items():
        out[name] = (out[name] * factor).astype(out[name].dtype)
    return out
```

```python
from contextlib import ExitStack

import concourse.bass as bass
from concourse import mybir

F32 = mybir.dt.float32
BF16 = mybir.dt.bfloat16
I32 = mybir.dt.int32
U32 = mybir.dt.uint32
U8 = mybir.dt.uint8
ALU = mybir.AluOpType
ACT = mybir.ActivationFunctionType
AX = mybir.AxisListType

P = 128
NEG = -1.0e30
RSQRT_SEED = 1597463007.0
EPS = 1e-5


class Tally:

    def __init__(self, eng, sem):
        self.eng, self.sem, self.base, self.local, self.loop = eng, sem, 0, 0, None

    def link(self, ins):
        self.local += 1
        ins.then_inc(self.sem, 1)
        value = self.base + self.local
        self.eng.wait_ge(self.sem, value if self.loop is None else self.loop + value)

    def enter(self, round_, per_round):
        self.base += self.local
        self.local, self.loop, self.per = 0, round_ * per_round, per_round

    def leave(self, rounds):
        assert self.local == self.per, (self.local, self.per)
        self.base += rounds * self.per
        self.local, self.loop = 0, None


def build(nc, x, ctx_in, mask, wq, bq, wk, bk, wv, bv, wo, bo, wr, rb, w1, w2, out, slots, pairs):
    B, S, D = x.shape
    NK = ctx_in.shape[1]
    H = 16
    DH = D // H
    E, _, F = w1.shape
    E1 = E + 1
    TT = S // P
    NT = B * TT
    NTOK = B * S
    HK = H * NK
    NCH = -(-HK // P)
    HKP = NCH * P
    G = 4
    HG = H // G
    GK = HG * NK
    FC = F // P
    TOPK = 2
    REGION = NTOK + P
    DEAD = E * REGION
    ROWS = DEAD + P
    NJ = NTOK * TOPK // P + E
    RW = D + 2
    QSCALE = float(DH) ** -0.5
    MAXT = NTOK // P
    LINKS = 61
    assert D == P and S % P == 0 and H * DH == D and NJ % 8 == 0
    NH3 = 3
    head0 = [min(P * c // NK, H - NH3) for c in range(NCH)]
    VC = NH3 * (DH + 1)

    es = ExitStack()
    with es:
        def sb(name, shape, dt=F32):
            return es.enter_context(nc.sbuf_tensor(name, shape, dt))

        def sem(name):
            return es.enter_context(nc.semaphore(name))

        x_sb = sb("x_sb", [P, NT * D])
        xb_sb = sb("xb_sb", [P, NT * D])
        base_sb = sb("base_sb", [P, NT * D])
        xn_sb = sb("xn_sb", [P, TT * D])
        xnT = sb("xnT", [P, TT * P])
        qT = sb("qT", [P, TT * P])
        ctx_sb = sb("ctx_sb", [NK, B, D])
        ctx3 = sb("ctx3", [P, B, 3, NK])
        kT = sb("kT", [P, B * NK])
        kbd = sb("kbd", [P, HG, NK])
        vbd = sb("vbd", [P, B, NCH, VC])
        vbias = sb("vbias", [P, NCH, NH3, DH])
        headrow3 = sb("headrow3", [P, NCH, NH3])
        headrow = sb("headrow", [P, NCH, H])
        hm16 = sb("hm16", [P, H])
        hm4 = sb("hm4", [P, HG])
        mask8 = sb("mask8", [P, B * NK], U8)
        negm = sb("negm", [P, B * GK], BF16)
        negb = sb("negb", [P, GK], BF16)
        ones_b = sb("ones_b", [P, P], BF16)
        upper_b = sb("upper_b", [P, P], BF16)
        ident = sb("ident", [P, P])
        wq_sb, wk_sb, wv_sb, wo_sb = (sb(n, [P, D]) for n in ("wq_sb", "wk_sb", "wv_sb", "wo_sb"))
        wr_sb = sb("wr_sb", [P, E1])
        w1_sb = sb("w1_sb", [P, E * F])
        w2_sb = sb("w2_sb", [P, E * F])
        bq_sb, bqs_sb, bk_sb = (sb(n, [P, 1]) for n in ("bq_sb", "bqs_sb", "bk_sb"))
        bv_sb, bo_sb = sb("bv_sb", [P, D]), sb("bo_sb", [P, D])
        rb_sb = sb("rb_sb", [P, E1])
        sc = sb("sc", [P, 2, HK])
        ex = sb("ex", [P, 2, HKP])
        exT = sb("exT", [P, 2, HKP])
        mx = sb("mx", [P, 2, H])
        av = sb("av", [P, 2, D])
        avT = sb("avT", [P, 2, P])
        rsum = sb("rsum", [P, H])
        st1 = sb("st1", [P, TT, 6])
        st2 = sb("st2", [P, TT, 6])
        mv1 = sb("mv1", [P, TT, 2])
        mv2 = sb("mv2", [P, TT, 2])
        nv, ny, nt_ = sb("nv", [P, TT]), sb("ny", [P, TT]), sb("nt_", [P, TT])
        rowsA, rowsB = sb("rowsA", [P, TT, RW]), sb("rowsB", [P, TT, RW])
        padrows = sb("padrows", [P, RW])
        x2nT = sb("x2nT", [P, TT * P])
        lgx = sb("lgx", [P, TT, E1 + 2])
        lex = sb("lex", [P, TT, E1 + 2])
        top = sb("top", [P, TT, 8])
        topi = sb("topi", [P, TT, 8], U32)
        topf = sb("topf", [P, TT, 2])
        lsum = sb("lsum", [P, TT, 1])
        gates = sb("gates", [P, TT, 2])
        oh = sb("oh", [P, 2, TT, E1])
        prod = sb("prod", [P, 2, TT, E1])
        chosen = sb("chosen", [P, TT, E1], BF16)
        cum = sb("cum", [P, TT + 1, E1])
        cumb = sb("cumb", [P, TT, E1], BF16)
        cumt = sb("cumt", [P, E1], BF16)
        rank = sb("rank", [P, TT, E1])
        slotf = sb("slotf", [P, 2, TT])
        slot = sb("slot", [P, 2, TT], U32)
        g8 = sb("g8", [P, 2, TT])
        iota9i, iota9 = sb("iota9i", [P, E1], I32), sb("iota9", [P, E1])
        ebasei, ebase = sb("ebasei", [P, E1], I32), sb("ebase", [P, E1])
        dest = sb("dest", [P, NT * 2], I32)
        cnt = sb("cnt", [P, E1])
        thr_i, thr = sb("thr_i", [P, MAXT], I32), sb("thr", [P, MAXT])
        tcmp = sb("tcmp", [P, E, MAXT])
        ntile, ntsum, gap = sb("ntile", [P, E]), sb("ntsum", [P, E]), sb("gap", [P, E])
        zero8 = sb("zero8", [P, E])
        jot_i, jot = sb("jot_i", [P, NJ], I32), sb("jot", [P, NJ])
        jcmp, jprod = sb("jcmp", [P, NJ, E]), sb("jprod", [P, NJ, E])
        jexp, jrow = sb("jexp", [P, NJ]), sb("jrow", [P, NJ])
        tab_w = sb("tab_w", [P, NJ], I32)
        tab_row = sb("tab_row", [P, NJ], I32)
        tab_pad = sb("tab_pad", [P, E], I32)
        padf = sb("padf", [P, E])
        zeros = sb("zeros", [P, 1024])
        R = 8
        xg = sb("xg", [P, R, RW])
        xgT = sb("xgT", [P, 2, P])
        hg = sb("hg", [P, 2, F])
        hT = sb("hT", [P, 2, F])
        yg = sb("yg", [P, 4, D])
        pair_sb = sb("pair_sb", [P, NT, 2 * D])
        out_sb = sb("out_sb", [P, NT, D])

        def psum(name, shape):
            return es.enter_context(nc.psum_tensor(name, shape, F32))

        ps_s = psum("ps_s", [P, G, 512])
        ps_t = [psum(f"ps_t{i}", [P, 512]) for i in range(2)]
        ps_av = psum("ps_av", [P, 512])
        ps_o = psum("ps_o", [P, 512])
        AV = ps_av[:, 0:H * (DH + 1)].rearrange("p (h d) -> p h d", d=DH + 1)
        LG = ps_av[:, 256:256 + TT * E1]
        RK = ps_av[:, 320:320 + TT * E1]
        TOT = ps_av[:, 384:384 + E1]
        ps_h, ps_ht = [ps_s[:, 0, :], ps_s[:, 1, :]], [ps_s[:, 2, :], ps_s[:, 3, :]]
        ps_xt, ps_y = [t[:, 0:P] for t in ps_t], [ps_av[:, 0:D], ps_o[:, 0:D]]

        ld_x = [sem(f"ld_x{b}") for b in range(B)]
        ld_ctx, ld_w, ld_small, ld_ffn = sem("ld_ctx"), sem("ld_w"), sem("ld_small"), sem("ld_ffn")
        zero_ready, pads_ready = sem("zero_ready"), sem("pads_ready")
        pre_done = sem("pre_done")
        consts = sem("consts")
        pool_c, dve_c = sem("pool_c"), sem("dve_c")
        bqs_ready = sem("bqs_ready")
        lone_waits = {e.engine: sem(f"lone_waits_{n}") for n, e in (("dve", nc.vector), ("pool", nc.gpsimd))}
        xn_ready, xb_ready = sem("xn_ready"), sem("xb_ready")
        k_full, kT_ready = sem("k_full"), sem("kT_ready")
        v_full, v_ready = sem("v_full"), sem("v_ready")
        kbd_ready = sem("kbd_ready")
        t_full, t_used = sem("t_full"), sem("t_used")
        s_full, s_used = sem("s_full"), sem("s_used")
        ex_ready = sem("ex_ready")
        av_full, av_ready = sem("av_full"), sem("av_ready")
        at_full, at_used = sem("at_full"), sem("at_used")
        o_full, x2_ready = sem("o_full"), sem("x2_ready")
        row_ready, rowb_ready = sem("row_ready"), sem("rowb_ready")
        lg_full, lg_used = sem("lg_full"), sem("lg_used")
        lgx_ready, lex_ready = sem("lgx_ready"), sem("lex_ready")
        chosen_ready, rk_full, rk_used = sem("chosen_ready"), sem("rk_full"), sem("rk_used")
        slot_ready = sem("slot_ready")
        sent = [sem(f"sent{t}") for t in range(TT)]
        cumt_ready, total_full, tab_ready = sem("cumt_ready"), sem("total_full"), sem("tab_ready")
        pads_done = sem("pads_done")
        got = [sem(f"got{u}") for u in range(R)]
        xt_full, xt_used = sem("xt_full"), sem("xt_used")
        h_full, h_used = sem("h_full"), sem("h_used")
        ht_full, ht_used = sem("ht_full"), sem("ht_used")
        y_full, y_used = sem("y_full"), sem("y_used")
        put = [sem(f"put{u}") for u in range(4)]
        pair_in = [sem(f"pair_in{b}") for b in range(B)]
        out_ready, stored = sem("out_ready"), sem("stored")

        block = es.enter_context(nc.Block())

        FILLS = {"T0": 0, "T1": 3, "xn": 6, "T2": 7, "x2n": 10, "q": 12, "T3": 13}
        ORDER = {"mid": list(range(16))}
        ORDER["first"] = [k for k in range(16) if k not in (0, 1, 2, 10, 11)]
        ORDER["last"] = [k for k in range(16) if k not in (6, 12)]
        ORDER["tail"] = [0, 1, 2, 10, 11]
        PRE_XN, PRE_Q = B, B + 1
        FIRST_FILL = B + 2
        MID_FILL = FIRST_FILL + len(ORDER["first"])
        LAST_FILL = MID_FILL + 16 * (B - 2)
        TAIL_FILL = LAST_FILL + len(ORDER["last"])

        def fill(kind, n, k):
            start = {"first": FIRST_FILL, "mid": MID_FILL, "last": LAST_FILL, "tail": TAIL_FILL}[kind]
            at = ORDER[kind].index(k)
            number = start + at
            if kind == "mid":
                return (n - 1) * 16 + number, number % 2
            return number, number % 2

        def stand_alone(eng):
            eng.sem_inc(lone_waits[eng.engine], 1)

        def batches(eng, step):
            for t in range(TT):
                step("first", 0, t)
            with eng.Fori(1, B - 1) as n:
                for t in range(TT):
                    step("mid", n, t)
            for t in range(TT):
                step("last", B - 1, t)

        @block.sync
        def _(sp):
            xv = x.rearrange("b (t p) d -> b p t d", p=P)
            x4 = x_sb[:, :].rearrange("p (b t d) -> p b t d", b=B, d=D)
            sp.dma_start(x4[:, 0], xv[0]).then_inc(ld_x[0], 16)
            sp.dma_start(ctx_sb[:, :, :], ctx_in.rearrange("b k d -> k b d")).then_inc(ld_ctx, 16)
            for dst, src in ((wk_sb, wk), (wq_sb, wq), (wv_sb, wv), (wo_sb, wo), (wr_sb, wr)):
                sp.dma_start(dst[:, :], src).then_inc(ld_w, 16)
            for b in range(1, B):
                sp.dma_start(x4[:, b], xv[b]).then_inc(ld_x[b], 16)
            sp.wait_ge(zero_ready, 1)
            pz = pairs.rearrange("(p r) d -> p (r d)", p=P)
            for i in range(pz.shape[1] // 1024):
                sp.dma_start(pz[:, i * 1024:(i + 1) * 1024], zeros[:, :]).then_inc(pre_done, 16)
            sp.wait_ge(pads_ready, 2)
            sp.dma_start(slots[DEAD:DEAD + P, :], padrows[:, :]).then_inc(pre_done, 16)
            sp.dma_start(w1_sb[:, :].rearrange("p (e f) -> p e f", e=E),
                         w1.rearrange("e d f -> d e f")).then_inc(ld_ffn, 16)
            sp.dma_start(w2_sb[:, :].rearrange("p (e c d) -> p e c d", e=E, c=FC),
                         w2.rearrange("e (c p) d -> p e c d", p=P)).then_inc(ld_ffn, 16)
            sp.wait_ge(tab_ready, 1)
            for e in range(E):
                row = sp.value_load(tab_pad[0:1, e:e + 1], min_val=0, max_val=DEAD - P)
                sp.dma_start(slots[bass.ds(row, P), :], padrows[:, :]).then_inc(pads_done, 16)
            sp.wait_ge(tab_ready, 2)
            sp.wait_ge(pads_done, 16 * E)
            sp.wait_ge(pre_done, 16 * (NTOK * TOPK // 1024 + 1))
            for t in range(TT):
                sp.wait_ge(sent[t], 32 * B)

            def load(j, u, first):
                if not first:
                    sp.wait_ge(put[u % 4], (j - R) * 4 + 16 - 4 * (u % 4))
                row = sp.value_load(tab_row[0:1, bass.ds(j, 1)], min_val=0, max_val=DEAD)
                sp.dma_start(xg[:, u, :], slots[bass.ds(row, P), :]).then_inc(got[u], 16)

            for u in range(R):
                load(u, u, True)
            with sp.Fori(1, NJ // R) as it:
                for u in range(R):
                    load(it * R + u, u, False)
            for u in range(4):
                sp.wait_ge(put[u], 16 * (NJ // 4))
            pv = pairs.rearrange("(t p c) d -> p t (c d)", p=P, c=2)
            for b in range(B):
                sp.dma_start(pair_sb[:, b * TT:(b + 1) * TT, :],
                             pv[:, b * TT:(b + 1) * TT, :]).then_inc(pair_in[b], 16)
            ov = out.rearrange("b (t p) d -> b p t d", p=P)
            for b in range(B):
                sp.wait_ge(out_ready, b + 1)
                sp.dma_start(ov[b], out_sb[:, b * TT:(b + 1) * TT, :]).then_inc(stored, 16)
            sp.wait_ge(stored, 16 * B)

        @block.gpsimd
        def _(pool):
            chain = Tally(pool, pool_c)
            pool.memset(zeros[:, :], 0.0).then_inc(zero_ready, 1)
            chain.link(pool.memset(ident[:, :], 0.0))
            pool.affine_select(out=ident[:, :], in_=ident[:, :], compare_op=ALU.not_equal, fill=1.0,
                               base=0, pattern=[[-1, P]], channel_multiplier=1).then_inc(consts, 1)
            chain.link(pool.memset(hm16[:, :], 1.0))
            chain.link(pool.affine_select(out=hm16[:, :], in_=hm16[:, :], compare_op=ALU.is_ge, fill=0.0,
                                          base=0, pattern=[[-DH, H]], channel_multiplier=1))
            pool.affine_select(out=hm16[:, :], in_=hm16[:, :], compare_op=ALU.is_ge, fill=0.0,
                               base=DH - 1, pattern=[[DH, H]], channel_multiplier=-1).then_inc(consts, 1)
            chain.link(pool.memset(headrow[:, :, :], 1.0))
            chain.link(pool.affine_select(out=headrow[:, :, :], in_=headrow[:, :, :], compare_op=ALU.is_ge,
                                          fill=0.0, base=0, pattern=[[P, NCH], [-NK, H]],
                                          channel_multiplier=1))
            pool.affine_select(out=headrow[:, :, :], in_=headrow[:, :, :], compare_op=ALU.is_ge, fill=0.0,
                               base=NK - 1, pattern=[[-P, NCH], [NK, H]],
                               channel_multiplier=-1).then_inc(consts, 1)
            pool.memset(ones_b[:, :], 1.0).then_inc(consts, 1)
            chain.link(pool.memset(upper_b[:, :], 1.0))
            pool.affine_select(out=upper_b[:, :], in_=upper_b[:, :], compare_op=ALU.is_gt, fill=0.0,
                               base=0, pattern=[[1, P]], channel_multiplier=-1).then_inc(consts, 1)
            pool.memset(ex[:, :, HK:HKP], 0.0).then_inc(consts, 1)
            pool.iota(iota9i[:, :], [[1, E1]], base=0, channel_multiplier=0).then_inc(consts, 1)
            pool.iota(ebasei[:, :], [[REGION, E1]], base=0, channel_multiplier=0).then_inc(consts, 1)
            pool.iota(dest[:, :], [[2 * P, NT], [1, 2]], base=0, channel_multiplier=2).then_inc(consts, 1)
            pool.iota(thr_i[:, :], [[P, MAXT]], base=0, channel_multiplier=0).then_inc(consts, 1)
            pool.iota(jot_i[:, :], [[1, NJ]], base=0, channel_multiplier=0).then_inc(consts, 1)
            pool.memset(padrows[:, 0:D + 1], 0.0).then_inc(pads_ready, 1)

            def xb(b):
                v = x_sb[:, b * TT * D:(b + 1) * TT * D].rearrange("p (t d) -> p t d", d=D)
                o = xb_sb[:, b * TT * D:(b + 1) * TT * D].rearrange("p (t d) -> p t d", d=D)
                pool.wait_ge(ld_x[b], 16)
                pool.tensor_tensor(o, v, bo_sb[:, :].unsqueeze(1).to_broadcast([P, TT, D]),
                                   ALU.add).then_inc(xb_ready, 1)

            def stage_k(n, first=False):
                if not first:
                    pool.wait_ge(s_full, n * 2 * TT)
                k = kT[:, bass.ds(n * NK, NK)].unsqueeze(1).to_broadcast([P, HG, NK])
                pool.tensor_tensor(kbd[:, :, :], k, hm4[:, :].unsqueeze(2).to_broadcast([P, HG, NK]),
                                   ALU.mult).then_inc(kbd_ready, 1)
                pool.tensor_copy(negb[:, :], negm[:, bass.ds(n * GK, GK)]).then_inc(kbd_ready, 1)

            def dispatch(m):
                pool.wait_ge(row_ready, m + 1)
                stand_alone(pool)
                pool.tensor_copy(rowsB[:, :, 0:D], rowsA[:, :, 0:D]).then_inc(rowb_ready, 1)
                pool.wait_ge(rowb_ready, m + 1)
                pool.wait_ge(slot_ready, m + 1)
                stand_alone(pool)
                for t in range(TT):
                    for c, rows in enumerate((rowsA, rowsB)):
                        pool.indirect_dma_start(
                            slots, bass.IndirectOffsetOnAxis(ap=slot[:, c, t:t + 1], axis=0),
                            rows[:, t, :], None, bounds_check=ROWS - 1,
                            oob_is_err=False).then_inc(sent[t], 16)

            pool.wait_ge(kT_ready, 3)
            stage_k(0, first=True)
            pool.wait_ge(ld_small, 16 * 5)
            for b in range(B):
                xb(b)
            stage_k(1)
            with pool.Fori(1, B - 1) as n:
                stage_k(n + 1)
                dispatch(n - 1)
            dispatch(B - 2)
            dispatch(B - 1)

            pool.wait_ge(pre_done, 16 * (NTOK * TOPK // 1024 + 1))

            def send_back(j, u):
                pool.wait_ge(y_used, j + 1)
                stand_alone(pool)
                pool.indirect_dma_start(
                    pairs, bass.IndirectOffsetOnAxis(ap=xg[:, u, D + 1:D + 2].bitcast(U32), axis=0),
                    yg[:, u % 4, :], None, bounds_check=NTOK * TOPK - 1,
                    oob_is_err=False).then_inc(put[u % 4], 16)

            with pool.Fori(0, NJ // R) as it:
                for u in range(R):
                    send_back(it * R + u, u)

        @block.scalar
        def _(act):
            for dst, src, n in ((bv_sb, bv, D), (bo_sb, bo, D), (rb_sb, rb, E1)):
                act.dma_start(dst[:, :], src.partition_broadcast(P)).then_inc(ld_small, 16)
            act.dma_start(mask8[:, :], mask.rearrange("b k -> (b k)").partition_broadcast(P)).then_inc(ld_small, 16)
            act.dma_start(bq_sb[:, :], bq.rearrange("(p o) -> p o", o=1)).then_inc(ld_small, 16)
            act.dma_start(bk_sb[:, :], bk.rearrange("(p o) -> p o", o=1)).then_inc(ld_ctx, 16)
            act.wait_ge(ld_small, 16 * 5)
            act.mul(bqs_sb[:, :], bq_sb[:, :], QSCALE).then_inc(bqs_ready, 1)

            for b in range(B):
                act.wait_ge(t_full, b + 1)
                for r in range(3):
                    i = act.copy(ctx3[:, b, r, :], ps_t[b % 2][:, 0:NK])
                i.then_inc(t_used, 1)

            def copy_fill(number, dst, src):
                act.wait_ge(t_full, number + 1)
                act.copy(dst, src).then_inc(t_used, 1)

            def store_q(number, bank):
                act.wait_ge(t_full, number + 1)
                act.activation(qT[:, :], ps_t[bank][:, :], ACT.Identity, bias=bqs_sb[:, 0:1],
                               scale=QSCALE).then_inc(t_used, 1)

            copy_fill(PRE_XN, xnT[:, :], ps_t[PRE_XN % 2][:, :])
            act.wait_ge(bqs_ready, 1)
            store_q(PRE_Q, PRE_Q % 2)

            def attn_t(i, par):
                act.wait_ge(at_full, i + 1)
                act.copy(avT[:, par, :], ps_o[:, 0:P]).then_inc(at_used, 1)

            def ex_t(kind, n, t, par):
                for p in range(3):
                    number, bank = fill(kind, n, FILLS[f"T{t}"] + p)
                    w = min(512, HKP - 512 * p)
                    copy_fill(number, exT[:, par, 512 * p:512 * p + w], ps_t[bank][:, 0:w])

            def x2n_t(kind, n):
                for h in range(2):
                    number, bank = fill(kind, n, FILLS["x2n"] + h)
                    copy_fill(number, x2nT[:, 2 * P * h:2 * P * (h + 1)], ps_t[bank][:, 0:2 * P])

            def router_exp(m):
                act.wait_ge(lgx_ready, m + 1)
                act.activation(lex[:, :, :], lgx[:, :, :], ACT.Exp).then_inc(lex_ready, 1)

            def step(kind, n, t):
                i = n * TT + t
                if kind != "first" or t >= 2:
                    attn_t(i - 2, t % 2)
                if t == 3 and kind != "last":
                    store_q(*fill(kind, n, FILLS["q"]))
                if kind != "first" or t >= 1:
                    ex_t(kind, n, t, (t + 1) % 2)
                if t == 1 and kind != "last":
                    number, bank = fill(kind, n, FILLS["xn"])
                    copy_fill(number, xnT[:, :], ps_t[bank][:, :])
                if t == 2 and kind != "first":
                    x2n_t(kind, n)
                if t == 3 and kind != "first":
                    router_exp(n - 1)
                act.wait_ge(s_used, i * 2 + 2)
                act.activation(ex[:, t % 2, 0:HK], sc[:, t % 2, :], ACT.Exp).then_inc(ex_ready, 1)

            act.wait_ge(consts, 6)
            batches(act, step)
            attn_t(NT - 2, 0)
            ex_t("tail", B, 0, 1)
            attn_t(NT - 1, 1)
            x2n_t("tail", B)
            router_exp(B - 1)

            def gelu(j, u):
                act.wait_ge(h_full, j + 1)
                if not isinstance(j, int) or j >= 2:
                    act.wait_ge(ht_full, j - 1)
                act.activation(hg[:, u % 2, :], ps_h[u % 2], ACT.Gelu).then_inc(h_used, 1)

            for u in range(R):
                gelu(u, u)
            with act.Fori(1, NJ // R) as it:
                for u in range(R):
                    gelu(it * R + u, u)

        @block.tensor
        def _(pe):
            def begin_fill(number):
                if not isinstance(number, int) or number >= 2:
                    pe.wait_ge(t_used, number - 1)

            pe.wait_ge(consts, 1)
            pe.wait_ge(ld_ctx, 32)
            for b in range(B):
                begin_fill(b)
                pe.transpose(ps_t[b % 2][:, 0:NK], ctx_sb[:, b, :], ident[0:NK, 0:NK]).then_inc(t_full, 1)
            pe.wait_ge(ld_w, 16 * 5)
            pe.wait_ge(t_used, B)
            pe.matmul(ps_av[:, 0:B * NK], wk_sb[:, :], ctx3[:, :, 0, :], start=True,
                      stop=True).then_inc(k_full, 1)

            def fill_xn(number, bank, batch1):
                begin_fill(number)
                pe.wait_ge(xn_ready, batch1)
                for t in range(TT):
                    i = pe.transpose(ps_t[bank][:, P * t:P * (t + 1)], xn_sb[:, D * t:D * (t + 1)], ident[:, :])
                i.then_inc(t_full, 1)

            def fill_q(number, bank, xn_number):
                begin_fill(number)
                pe.wait_ge(t_used, xn_number + 1)
                pe.matmul(ps_t[bank][:, :], wq_sb[:, :], xnT[:, :], start=True, stop=True).then_inc(t_full, 1)

            fill_xn(PRE_XN, PRE_XN % 2, 1)
            fill_q(PRE_Q, PRE_Q % 2, PRE_XN)

            for b in range(B):
                rep = ctx3[:, b, :, :].rearrange("p r k -> p (r k)")
                for c in range(NCH):
                    off = P * c % NK
                    i = pe.matmul(ps_s[:, b, NH3 * DH * c:NH3 * DH * (c + 1)], rep[:, off:off + P],
                                  wv_sb[:, DH * head0[c]:DH * (head0[c] + NH3)], start=True, stop=True)
                i.then_inc(v_full, 1)

            def scores(kind, n, t):
                i = n * TT + t
                if t == 0:
                    if kind == "first":
                        pe.wait_ge(t_used, PRE_Q + 1)
                        pe.wait_ge(v_ready, B)
                        pe.wait_ge(consts, 4)
                    else:
                        pe.wait_ge(t_used, Q_OF_0 + 1 + (n - 1) * 16)
                    pe.wait_ge(kbd_ready, n * 2 + 2)
                for half in range(2):
                    if kind != "first" or t > 0:
                        pe.wait_ge(s_used, i * 2 - 1 + half)
                    for g in (2 * half, 2 * half + 1):
                        r = slice(32 * g, 32 * g + 32)
                        pe.matmul(ps_s[:, g, 0:GK], qT[r, P * t:P * (t + 1)],
                                  kbd[r, :, :].rearrange("p h k -> p (h k)"), start=True, stop=False)
                        m = pe.matmul(ps_s[:, g, 0:GK], ones_b[32 * g:32 * g + 1, :], negb[32 * g:32 * g + 1, :],
                                      start=False, stop=True)
                    m.then_inc(s_full, 1)

            def attn_t(i, par, first):
                pe.wait_ge(av_ready, i + 1)
                if not first:
                    pe.wait_ge(x2_ready, i)
                pe.transpose(ps_o[:, 0:P], av[:, par, :], ident[:, :]).then_inc(at_full, 1)

            def project(i, par):
                pe.wait_ge(at_used, i + 1)
                pe.matmul(ps_o[:, P:P + D], avT[:, par, :], wo_sb[:, :], start=True,
                          stop=True).then_inc(o_full, 1)

            def ex_t(kind, n, t, i, par):
                pe.wait_ge(ex_ready, i + 1)
                for p in range(3):
                    number, bank = fill(kind, n, FILLS[f"T{t}"] + p)
                    begin_fill(number)
                    for c in range(4 * p, min(4 * p + 4, NCH)):
                        m = pe.transpose(ps_t[bank][:, P * (c % 4):P * (c % 4 + 1)], ex[:, par, P * c:P * (c + 1)],
                                         ident[:, :])
                    m.then_inc(t_full, 1)

            def values(kind, n, t, i, b, par):
                if not (isinstance(i, int) and i == 0):
                    pe.wait_ge(av_ready, i)
                for p in range(3):
                    number, _ = fill(kind, n, FILLS[f"T{t}"] + p)
                    pe.wait_ge(t_used, number + 1)
                    for c in range(4 * p, min(4 * p + 4, NCH)):
                        v = vflat[:, bass.ds((b * NCH + c) * VC, VC)]
                        m = pe.matmul(ps_av[:, (DH + 1) * head0[c]:(DH + 1) * head0[c] + VC],
                                      exT[:, par, P * c:P * (c + 1)], v, start=c == 0, stop=c == NCH - 1,
                                      skip_group_check=True)
                m.then_inc(av_full, 1)

            def fill_x2n(kind, n, m):
                pe.wait_ge(row_ready, m + 1)
                for h in range(2):
                    number, bank = fill(kind, n, FILLS["x2n"] + h)
                    begin_fill(number)
                    for t in (2 * h, 2 * h + 1):
                        x_ = pe.transpose(ps_t[bank][:, P * (t % 2):P * (t % 2 + 1)], rowsA[:, t, 0:D], ident[:, :])
                    x_.then_inc(t_full, 1)

            def logits(kind, n, m):
                number, _ = fill(kind, n, FILLS["x2n"] + 1)
                pe.wait_ge(t_used, number + 1)
                for t in range(TT):
                    x_ = pe.matmul(LG[:, E1 * t:E1 * (t + 1)], x2nT[:, P * t:P * (t + 1)], wr_sb[:, :],
                                   start=True, stop=True)
                x_.then_inc(lg_full, 1)

            def ranks(m):
                pe.wait_ge(chosen_ready, m + 1)
                pe.matmul(RK, upper_b[:, :], chosen[:, :, :].rearrange("p t e -> p (t e)"), start=True, stop=False)
                pe.matmul(RK, ones_b[:, :], cumb[:, :, :].rearrange("p t e -> p (t e)"), start=False,
                          stop=True).then_inc(rk_full, 1)

            vflat = vbd[:, :, :, :].rearrange("p b c v -> p (b c v)")
            Q_OF_0, _ = fill("first", 0, FILLS["q"])

            def step(kind, n, t):
                i = n * TT + t
                if t == 3 and kind != "first":
                    pe.wait_ge(av_ready, i - 1)
                    logits(kind, n, n - 1)
                scores(kind, n, t)
                if kind != "first" or t >= 2:
                    attn_t(i - 2, t % 2, kind == "first" and t == 2)
                if t == 3 and kind != "last":
                    number, bank = fill(kind, n, FILLS["q"])
                    fill_q(number, bank, fill(kind, n, FILLS["xn"])[0])
                if kind != "first" or t >= 1:
                    ex_t(kind, n, t, i - 1, (t + 1) % 2)
                    if t == 3 and kind != "first":
                        pe.wait_ge(lg_used, n)
                    if t == 0 and kind != "first":
                        pe.wait_ge(rk_used, n)
                    values(kind, n, t, i - 1, n if t else n - 1, (t + 1) % 2)
                if kind != "first" or t >= 2:
                    project(i - 2, t % 2)
                if t == 1 and kind != "last":
                    fill_xn(*fill(kind, n, FILLS["xn"]), n + 2)
                if t == 2 and kind != "first":
                    fill_x2n(kind, n, n - 1)
                if t == 3 and kind != "first":
                    pe.wait_ge(av_ready, i)
                    ranks(n - 1)

            pe.wait_ge(kT_ready, 1)
            batches(pe, step)
            attn_t(NT - 2, 0, False)
            ex_t("tail", B, 0, NT - 1, 1)
            pe.wait_ge(rk_used, B)
            values("tail", B, 0, NT - 1, B - 1, 1)
            project(NT - 2, 0)
            attn_t(NT - 1, 1, False)
            project(NT - 1, 1)
            fill_x2n("tail", B, B - 1)
            pe.wait_ge(av_ready, NT)
            logits("tail", B, B - 1)
            pe.wait_ge(lg_used, B)
            ranks(B - 1)
            pe.wait_ge(rk_used, B + 1)
            pe.wait_ge(cumt_ready, 1)
            pe.matmul(TOT, ones_b[:, :], cumt[:, :], start=True, stop=True).then_inc(total_full, 1)

            pe.wait_ge(tab_ready, 2)
            pe.wait_ge(ld_ffn, 32)

            def expert_of(j):
                return pe.value_load(tab_w[0:1, bass.ds(j, 1)], min_val=0, max_val=(E - 1) * F)

            def gather_t(j, u, it):
                pe.wait_ge(got[u], it * 16 + 16)
                if not isinstance(j, int) or j >= 2:
                    pe.wait_ge(xt_used, j - 1)
                pe.transpose(ps_xt[u % 2], xg[:, u, 0:D], ident[:, :]).then_inc(xt_full, 1)

            def up(j, par):
                e = expert_of(j)
                pe.wait_ge(xt_used, j + 1)
                if not isinstance(j, int) or j >= 2:
                    pe.wait_ge(h_used, j - 1)
                pe.matmul(ps_h[par], xgT[:, par, :], w1_sb[:, bass.ds(e, F)], start=True,
                          stop=True).then_inc(h_full, 1)

            def hidden_t(j, par):
                pe.wait_ge(h_used, j + 1)
                if not isinstance(j, int) or j >= 2:
                    pe.wait_ge(ht_used, j - 1)
                for c in range(FC):
                    m = pe.transpose(ps_ht[par][:, P * c:P * (c + 1)], hg[:, par, P * c:P * (c + 1)], ident[:, :])
                m.then_inc(ht_full, 1)

            def down(j, par):
                e = expert_of(j)
                pe.wait_ge(ht_used, j + 1)
                if not isinstance(j, int) or j >= 2:
                    pe.wait_ge(y_used, j - 1)
                for c in range(FC):
                    m = pe.matmul(ps_y[par], hT[:, par, P * c:P * (c + 1)], w2_sb[:, bass.ds(e + P * c, D)],
                                  start=c == 0, stop=c == FC - 1)
                m.then_inc(y_full, 1)

            for j in range(NJ + 3):
                if j == R:
                    with pe.Fori(1, NJ // R) as it:
                        for u in range(R):
                            jj = it * R + u
                            gather_t(jj, u, it)
                            up(jj - 1, (u + 1) % 2)
                            hidden_t(jj - 2, u % 2)
                            down(jj - 3, (u + 1) % 2)
                if R <= j < NJ:
                    continue
                if j < NJ:
                    gather_t(j, j, 0)
                if 0 <= j - 1 < NJ:
                    up(j - 1, (j - 1) % 2)
                if 0 <= j - 2 < NJ:
                    hidden_t(j - 2, j % 2)
                if 0 <= j - 3 < NJ:
                    down(j - 3, (j - 3) % 2)

        @block.vector
        def _(dve):
            chain = Tally(dve, dve_c)
            link = chain.link

            def rsqrt(var):
                link(dve.tensor_scalar(nv[:, :], var, EPS, None, ALU.add))
                link(dve.tensor_scalar(ny[:, :].bitcast(I32), nv[:, :].bitcast(I32), -0.5, RSQRT_SEED,
                                       ALU.mult, ALU.add))
                for _ in range(3):
                    link(dve.tensor_tensor(nt_[:, :], ny[:, :], ny[:, :], ALU.mult))
                    link(dve.scalar_tensor_tensor(nt_[:, :], nt_[:, :], -0.5, nv[:, :], ALU.mult, ALU.mult))
                    link(dve.scalar_tensor_tensor(ny[:, :], nt_[:, :], 1.5, ny[:, :], ALU.add, ALU.mult))

            def norm1(n):
                stand_alone(dve)
                for t in range(TT):
                    i = dve.bn_stats(st1[:, t, :], x_sb[:, bass.ds((n * TT + t) * D, D)])
                link(i)
                stand_alone(dve)
                for t in range(TT):
                    i = dve.bn_aggr(mv1[:, t, :], st1[:, t, :])
                link(i)
                rsqrt(mv1[:, :, 1])
                for t in range(TT):
                    i = dve.tensor_scalar(xn_sb[:, D * t:D * (t + 1)], x_sb[:, bass.ds((n * TT + t) * D, D)],
                                          mv1[:, t, 0:1], ny[:, t:t + 1], ALU.subtract, ALU.mult)
                i.then_inc(xn_ready, 1)

            dve.wait_ge(ld_x[0], 16)
            norm1(0)
            dve.wait_ge(k_full, 1)
            dve.tensor_scalar(kT[:, :], ps_av[:, 0:B * NK], bk_sb[:, 0:1], None, ALU.add).then_inc(kT_ready, 1)
            dve.wait_ge(consts, 2)
            dve.tensor_reduce(hm4[:, :], hm16[:, :].rearrange("p (g j) -> p j g", g=G), AX.X,
                              ALU.add).then_inc(kT_ready, 1)
            dve.wait_ge(ld_small, 16 * 5)
            m4 = mask8[:, :].rearrange("p (b k) -> p b k", b=B).unsqueeze(2).to_broadcast([P, B, HG, NK])
            dve.tensor_scalar(negm[:, :].rearrange("p (b h k) -> p b h k", b=B, h=HG), m4, NEG, None,
                              ALU.mult).then_inc(kT_ready, 1)
            dve.wait_ge(consts, 3)
            for c in range(NCH):
                i = dve.tensor_copy(headrow3[:, c, :], headrow[:, c, head0[c]:head0[c] + NH3])
            link(i)
            for c in range(NCH):
                bv3 = bv_sb[:, DH * head0[c]:DH * (head0[c] + NH3)].rearrange("p (h d) -> p h d", d=DH)
                i = dve.tensor_tensor(vbias[:, c, :, :], bv3,
                                      headrow3[:, c, :].unsqueeze(2).to_broadcast([P, NH3, DH]), ALU.mult)
            link(i)
            CH3 = NCH * NH3
            hr = headrow3[:, :, :].rearrange("p c h -> p (c h)")
            vb2 = vbias[:, :, :, :].rearrange("p c h d -> p (c h) d")
            for b in range(B):
                dve.wait_ge(v_full, b + 1)
                o = vbd[:, b, :, :].rearrange("p c (h d) -> p (c h) d", d=DH + 1)
                link(dve.tensor_tensor(o[:, :, 0:DH],
                                       ps_s[:, b, 0:CH3 * DH].rearrange("p (c d) -> p c d", d=DH),
                                       hr.unsqueeze(2).to_broadcast([P, CH3, DH]), ALU.mult))
                dve.tensor_copy(o[:, :, DH], hr)
                dve.tensor_tensor(o[:, :, 0:DH], o[:, :, 0:DH], vb2, ALU.add).then_inc(v_ready, 1)
            dve.wait_ge(consts, 11)
            dve.tensor_copy(iota9[:, :], iota9i[:, :]).then_inc(rk_used, 1)
            dve.memset(cum[:, TT, :], 0.0)
            dve.memset(zero8[:, :], 0.0)
            dve.tensor_copy(thr[:, :], thr_i[:, :])
            dve.tensor_copy(jot[:, :], jot_i[:, :])
            dve.tensor_scalar(padrows[:, D + 1:D + 2].bitcast(I32), dest[:, 0:1], 0, NTOK * TOPK, ALU.mult,
                              ALU.add).then_inc(pads_ready, 1)
            link(dve.tensor_copy(ebase[:, :], ebasei[:, :]))
            link(dve.tensor_scalar(ebase[:, E:E1], ebase[:, E:E1], float(P), None, ALU.add))
            for b in range(1, B):
                dve.wait_ge(ld_x[b], 16)
            dve.wait_ge(xb_ready, B)

            def less_max(kind, n, t):
                i = n * TT + t
                par = t % 2
                for half in range(2):
                    dve.wait_ge(s_full, i * 2 + half + 1)
                    s = ps_s[:, 2 * half:2 * half + 2, 0:GK].rearrange("p g (h k) -> p g h k", k=NK)
                    m = mx[:, par, 8 * half:8 * half + 8]
                    link(dve.tensor_reduce(m, s, AX.X, ALU.max))
                    if half == 0 and (kind != "first" or t >= 2):
                        dve.wait_ge(ex_ready, i - 1)
                    o = sc[:, par, 2 * GK * half:2 * GK * (half + 1)]
                    dve.tensor_tensor(o.rearrange("p (g h k) -> p g h k", g=2, k=NK), s,
                                      m.rearrange("p (g h) -> p g h", g=2).unsqueeze(3)
                                      .to_broadcast([P, 2, HG, NK]), ALU.subtract).then_inc(s_used, 1)

            def residual(i, t):
                dve.wait_ge(o_full, i + 1)
                o = base_sb[:, bass.ds(i * D, D)]
                x2 = dve.tensor_tensor(o, ps_o[:, P:P + D], xb_sb[:, bass.ds(i * D, D)], ALU.add)
                x2.then_inc(x2_ready, 1)
                dve.wait_ge(x2_ready, i + 1)
                stand_alone(dve)
                link(dve.bn_stats(st2[:, t, :], o))
                stand_alone(dve)
                link(dve.bn_aggr(mv2[:, t, :], st2[:, t, :]))

            def weigh(i, par):
                dve.wait_ge(av_full, i + 1)
                link(dve.reciprocal(rsum[:, :], AV[:, :, DH]))
                dve.tensor_tensor(av[:, par, :].rearrange("p (h d) -> p h d", d=DH), AV[:, :, 0:DH],
                                  rsum[:, :].unsqueeze(2).to_broadcast([P, H, DH]),
                                  ALU.mult).then_inc(av_ready, 1)

            def norm2(m):
                rsqrt(mv2[:, :, 1])
                for t in range(TT):
                    if not (isinstance(m, int) and m == 0):
                        dve.wait_ge(sent[t], m * 32)
                    i = dve.tensor_scalar(rowsA[:, t, 0:D], base_sb[:, bass.ds((m * TT + t) * D, D)],
                                          mv2[:, t, 0:1], ny[:, t:t + 1], ALU.subtract, ALU.mult)
                i.then_inc(row_ready, 1)

            def choose(m):
                dve.wait_ge(lg_full, m + 1)
                i = dve.tensor_tensor(lgx[:, :, 0:E1], LG.rearrange("p (t e) -> p t e", t=TT),
                                      rb_sb[:, :].unsqueeze(1).to_broadcast([P, TT, E1]), ALU.add)
                i.then_inc(lg_used, 1)
                dve.wait_ge(lg_used, m + 1)
                stand_alone(dve)
                for t in range(TT):
                    i = dve.max(top[:, t, :], lgx[:, t, 0:E1])
                link(i)
                stand_alone(dve)
                for t in range(TT):
                    dve.max_index(topi[:, t, :], top[:, t, :], lgx[:, t, 0:E1])
                link(dve.tensor_copy(lgx[:, :, E1:E1 + 2], top[:, :, 0:2]))
                dve.tensor_tensor(lgx[:, :, :], lgx[:, :, :], top[:, :, 0:1].to_broadcast([P, TT, E1 + 2]),
                                  ALU.subtract).then_inc(lgx_ready, 1)
                link(dve.tensor_copy(topf[:, :, :], topi[:, :, 0:2]))
                for c in range(2):
                    i = dve.tensor_tensor(oh[:, c, :, :], iota9[:, :].unsqueeze(1).to_broadcast([P, TT, E1]),
                                          topf[:, :, c:c + 1].to_broadcast([P, TT, E1]), ALU.is_equal)
                link(i)
                dve.tensor_copy(cum[:, 0, :], cum[:, TT, :])
                link(dve.tensor_tensor(chosen[:, :, :], oh[:, 0, :, :], oh[:, 1, :, :], ALU.add))
                for t in range(TT):
                    link(dve.tensor_tensor(cum[:, t + 1, :], cum[:, t, :], chosen[:, t, :], ALU.add))
                dve.tensor_copy(cumb[:, :, :], cum[:, 0:TT, :]).then_inc(chosen_ready, 1)

            def place(m):
                dve.wait_ge(rk_full, m + 1)
                i = dve.tensor_tensor(rank[:, :, :], RK.rearrange("p (t e) -> p t e", t=TT),
                                      ebase[:, :].unsqueeze(1).to_broadcast([P, TT, E1]), ALU.add)
                i.then_inc(rk_used, 1)
                dve.wait_ge(rk_used, m + 2)
                for c in range(2):
                    i = dve.tensor_tensor(prod[:, c, :, :], oh[:, c, :, :], rank[:, :, :], ALU.mult)
                link(i)
                link(dve.tensor_reduce(slotf[:, :, :], prod[:, :, :, :], AX.X, ALU.add))
                dve.tensor_copy(slot[:, :, :], slotf[:, :, :])
                dve.wait_ge(lex_ready, m + 1)
                link(dve.tensor_reduce(lsum[:, :, :], lex[:, :, 0:E1], AX.X, ALU.add))
                link(dve.reciprocal(lsum[:, :, :], lsum[:, :, :]))
                link(dve.tensor_tensor(gates[:, :, :], lex[:, :, E1:E1 + 2], lsum[:, :, :].to_broadcast([P, TT, 2]),
                                       ALU.mult))
                to = dest[:, bass.ds(m * TT * 2, TT * 2)].rearrange("p (t c) -> p t c", c=2)
                for c, rows in enumerate((rowsA, rowsB)):
                    dve.tensor_copy(rows[:, :, D:D + 1], gates[:, :, c:c + 1])
                    i = dve.tensor_copy(rows[:, :, D + 1:D + 2].bitcast(I32), to[:, :, c:c + 1])
                i.then_inc(slot_ready, 1)
                link(dve.tensor_tensor(g8[:, :, :], oh[:, :, :, E],
                                       gates[:, :, :].rearrange("p t c -> p c t"), ALU.mult))
                link(dve.tensor_tensor(g8[:, 0, :], g8[:, 0, :], g8[:, 1, :], ALU.add))
                for t in range(TT):
                    o = base_sb[:, bass.ds((m * TT + t) * D, D)]
                    i = dve.scalar_tensor_tensor(o, rowsA[:, t, 0:D], g8[:, 0, t:t + 1], o, ALU.mult, ALU.add)
                link(i)

            def step(kind, n, t):
                i = n * TT + t
                if t == 3 and kind != "first":
                    choose(n - 1)
                less_max(kind, n, t)
                if kind != "first" or t >= 2:
                    residual(i - 2, (t + 2) % 4)
                if kind != "first" or t >= 1:
                    weigh(i - 1, (t + 1) % 2)
                if t == 0 and kind != "last":
                    norm1(n + 1)
                if t == 1 and kind != "first":
                    norm2(n - 1)
                if t == 3 and kind != "first":
                    place(n - 1)

            def steps():
                for t in range(TT):
                    step("first", 0, t)
                chain_at = chain.local
                with dve.Fori(1, B - 1) as n:
                    chain.enter(n - 1, LINKS)
                    for t in range(TT):
                        step("mid", n, t)
                    chain.leave(B - 2)
                for t in range(TT):
                    step("last", B - 1, t)

            steps()
            residual(NT - 2, 2)
            weigh(NT - 1, 1)
            residual(NT - 1, 3)
            norm2(B - 1)
            choose(B - 1)
            dve.tensor_copy(cumt[:, :], cum[:, TT, :]).then_inc(cumt_ready, 1)
            place(B - 1)

            dve.wait_ge(total_full, 1)
            link(dve.tensor_copy(cnt[:, :], TOT))
            dve.tensor_tensor(tab_pad[:, :], cnt[:, 0:E], ebase[:, 0:E], ALU.add).then_inc(tab_ready, 1)
            link(dve.tensor_tensor(tcmp[:, :, :], cnt[:, 0:E].unsqueeze(2).to_broadcast([P, E, MAXT]),
                                   thr[:, :].unsqueeze(1).to_broadcast([P, E, MAXT]), ALU.is_gt))
            link(dve.tensor_reduce(ntile[:, :], tcmp[:, :, :], AX.X, ALU.add))
            dve.tensor_scalar(gap[:, :], ntile[:, :], -float(P), float(REGION), ALU.mult, ALU.add)
            link(dve.tensor_tensor_scan(ntsum[:, :], ntile[:, :], zero8[:, :], 0.0, ALU.add, ALU.add))
            link(dve.tensor_tensor(jcmp[:, :, :], jot[:, :].unsqueeze(2).to_broadcast([P, NJ, E]),
                                   ntsum[:, :].unsqueeze(1).to_broadcast([P, NJ, E]), ALU.is_ge))
            dve.tensor_reduce(jexp[:, :], jcmp[:, :, :], AX.X, ALU.add)
            link(dve.tensor_tensor(jprod[:, :, :], jcmp[:, :, :], gap[:, :].unsqueeze(1).to_broadcast([P, NJ, E]),
                                   ALU.mult))
            link(dve.tensor_reduce(jrow[:, :], jprod[:, :, :], AX.X, ALU.add))
            dve.tensor_scalar(tab_w[:, :], jexp[:, :], float(E - 1), float(F), ALU.min, ALU.mult)
            link(dve.scalar_tensor_tensor(jrow[:, :], jot[:, :], float(P), jrow[:, :], ALU.mult, ALU.add))
            dve.tensor_scalar(tab_row[:, :], jrow[:, :], float(DEAD), None, ALU.min).then_inc(tab_ready, 1)

            def take_rows(j, par):
                dve.wait_ge(xt_full, j + 1)
                dve.tensor_copy(xgT[:, par, :], ps_xt[par]).then_inc(xt_used, 1)

            def take_hidden(j, par):
                dve.wait_ge(ht_full, j + 1)
                dve.tensor_copy(hT[:, par, :], ps_ht[par]).then_inc(ht_used, 1)

            def take_result(j, slot8, quads):
                dve.wait_ge(y_full, j + 1)
                if not (isinstance(quads, int) and quads == 0):
                    dve.wait_ge(put[slot8 % 4], quads * 16)
                dve.tensor_scalar(yg[:, slot8 % 4, :], ps_y[slot8 % 2], xg[:, slot8, D:D + 1], None,
                                  ALU.mult).then_inc(y_used, 1)

            for j in range(NJ + 3):
                if j == R:
                    with dve.Fori(1, NJ // R) as it:
                        for u in range(R):
                            jj = it * R + u
                            take_rows(jj, u % 2)
                            take_hidden(jj - 2, u % 2)
                            quads = it * 2 + (u - 3) // 4
                            take_result(jj - 3, (u - 3) % 8, quads)
                if R <= j < NJ:
                    continue
                if j < NJ:
                    take_rows(j, j % 2)
                if 0 <= j - 2 < NJ:
                    take_hidden(j - 2, j % 2)
                if 0 <= j - 3 < NJ:
                    take_result(j - 3, (j - 3) % R, (j - 3) // 4)

            for b in range(B):
                dve.wait_ge(pair_in[b], 16)
                r = slice(b * TT, (b + 1) * TT)
                link(dve.tensor_tensor(out_sb[:, r, :], pair_sb[:, r, 0:D], pair_sb[:, r, D:2 * D], ALU.add))
                dve.tensor_tensor(out_sb[:, r, :], out_sb[:, r, :],
                                  base_sb[:, b * TT * D:(b + 1) * TT * D].rearrange("p (t d) -> p t d", d=D),
                                  ALU.add).then_inc(out_ready, 1)


_INS = ["x", "ctx_1024", "mask_BxS2_bk0", "L0_xattn_Wq", "L0_xattn_bq", "L0_xattn_Wk", "L0_xattn_bk",
        "L0_xattn_Wv", "L0_xattn_bv", "L0_xattn_Wo", "L0_xattn_bo", "L0_ffn_router_w", "L0_ffn_router_b",
        "L0_ffn_w1", "L0_ffn_w2"]


def kernel(**inputs):
    import numpy as _np
    import concourse.bacc as _bacc
    from concourse import mybir as _mybir
    from concourse.bass_utils import run_bass_kernel_spmd as _run

    nc = _bacc.Bacc("TRN2", target_bir_lowering=False, num_devices=1)
    arrays, args = {}, []
    for name in _INS:
        a = _np.ascontiguousarray(inputs[name])
        arrays[f"in_{name}"] = a
        args.append(nc.dram_tensor(f"in_{name}", a.shape, _mybir.dt.from_np(a.dtype), kind="ExternalInput").ap())
    x = inputs["x"]
    tokens, width, experts = x.shape[0] * x.shape[1], x.shape[2], inputs["L0_ffn_w1"].shape[0]
    f32 = _mybir.dt.float32
    args.append(nc.dram_tensor("out", tuple(x.shape), f32, kind="ExternalOutput").ap())
    args.append(nc.dram_tensor("slots", (experts * (tokens + 128) + 128, width + 2), f32, kind="Internal").ap())
    args.append(nc.dram_tensor("pairs", (2 * tokens, width), f32, kind="Internal").ap())
    build(nc, *args)
    r = _run(nc, [arrays], core_ids=[0])
    return r.results[0]["out"]
```

```python
from contextlib import ExitStack

import concourse.bass as bass
from concourse import mybir

F32 = mybir.dt.float32
BF16 = mybir.dt.bfloat16
I32 = mybir.dt.int32
U32 = mybir.dt.uint32
U8 = mybir.dt.uint8
ALU = mybir.AluOpType
ACT = mybir.ActivationFunctionType
AX = mybir.AxisListType

P = 128
EPS = 1e-5


class Tally:

    def __init__(self, eng, sem):
        self.eng, self.sem, self.base, self.local, self.loop = eng, sem, 0, 0, None

    def link(self, ins):
        self.local += 1
        ins.then_inc(self.sem, 1)
        value = self.base + self.local
        self.eng.wait_ge(self.sem, value if self.loop is None else self.loop + value)

    def enter(self, round_, per_round):
        self.base += self.local
        self.local, self.loop, self.per = 0, round_ * per_round, per_round

    def leave(self, rounds):
        assert self.local == self.per, (self.local, self.per)
        self.base += rounds * self.per
        self.local, self.loop = 0, None


def build(nc, x, ctx_in, mask, wq, bq, wk, bk, wv, bv, wo, bo, wr, rb, w1, w2, out, slots, pairs):
    B, S, D = x.shape
    NK = ctx_in.shape[1]
    H = 16
    DH = D // H
    E, _, F = w1.shape
    E1 = E + 1
    TT = S // P
    NT = B * TT
    NTOK = B * S
    HK = H * NK
    NCH = -(-HK // P)
    HKP = NCH * P
    G = 4
    HG = H // G
    GK = HG * NK
    FC = F // P
    TOPK = 2
    REGION = NTOK + P
    DEAD = E * REGION
    ROWS = DEAD + P
    NJ = NTOK * TOPK // P + E
    RW = D + 2
    QSCALE = float(DH) ** -0.5
    MAXT = NTOK // P
    LINKS = 28
    CHUNKS = [(b * TT, (b + 1) * TT) for b in range(B - 1)] + [(NT - TT, NT - 2), (NT - 2, NT)]
    assert D == P and S % P == 0 and H * DH == D and NJ % 8 == 0
    PIECES = [(0, 3), (3, 7), (7, NCH)]
    assert all(z - a <= 4 for a, z in PIECES)
    NH3 = 3
    head0 = [min(P * c // NK, H - NH3) for c in range(NCH)]
    VB = B * NH3 * (DH + 1)
    VC = 11 * (DH + 1)

    es = ExitStack()
    with es:
        def sb(name, shape, dt=F32):
            return es.enter_context(nc.sbuf_tensor(name, shape, dt))

        def sem(name):
            return es.enter_context(nc.semaphore(name))

        x_sb = sb("x_sb", [P, NT * D])
        xb_sb = sb("xb_sb", [P, NT * D])
        base_sb = sb("base_sb", [P, NT * D])
        xn_sb = sb("xn_sb", [P, TT * D])
        xnT = sb("xnT", [P, TT * P])
        qT = sb("qT", [P, TT * P])
        ctx_sb = sb("ctx_sb", [NK, B, D])
        ctxT = sb("ctxT", [P, B, NK])
        kT = sb("kT", [P, B * NK])
        kbd = sb("kbd", [P, HG, NK])
        vbd = sb("vbd", [P, B, NCH, VC])
        v_sb = sb("v_sb", [NK, B, H, DH + 1])
        repeat = sb("repeat", [NK, HKP])
        vtail = sb("vtail", [P, 2 * B * NH3 * (DH + 1)])
        headrow3 = sb("headrow3", [P, NCH, NH3, DH + 1])
        headrow = sb("headrow", [P, NCH, H])
        hm16 = sb("hm16", [P, H])
        hm4 = sb("hm4", [P, HG])
        mask8 = sb("mask8", [P, B * NK], U8)
        maskf, valid = sb("maskf", [P, B * NK]), sb("valid", [P, B * NK])
        nvalid, kmean = sb("nvalid", [P, B]), sb("kmean", [P, B])
        valid_own, validT = sb("valid_own", [NK, B, NK]), sb("validT", [NK, B])
        ones_b = sb("ones_b", [P, P], BF16)
        upper_b = sb("upper_b", [P, P], BF16)
        ident = sb("ident", [P, P])
        wq_sb, wk_sb, wv_sb, wo_sb = (sb(n, [P, D]) for n in ("wq_sb", "wk_sb", "wv_sb", "wo_sb"))
        WR = 64
        wr_sb = sb("wr_sb", [P, WR])
        w1_sb = sb("w1_sb", [P, E * F])
        w2_sb = sb("w2_sb", [P, E * F])
        bq_sb, bqs_sb, bk_sb = (sb(n, [P, 1]) for n in ("bq_sb", "bqs_sb", "bk_sb"))
        bv_sb, bo_sb = sb("bv_sb", [P, D]), sb("bo_sb", [P, D])
        rb_sb = sb("rb_sb", [P, E1])
        sc = sb("sc", [P, 2, HK])
        ex = sb("ex", [P, 2, HKP])
        exT = sb("exT", [P, 2, HKP])
        mx = sb("mx", [P, 2, H])
        av = sb("av", [P, 2, D])
        avT = sb("avT", [P, 2, P])
        rsum = sb("rsum", [P, H])
        st1 = sb("st1", [P, NT, 6])
        mv1 = sb("mv1", [P, NT, 2])
        veps1, rstd1, seed1, nt1, shift1 = (sb(n, [P, NT]) for n in ("veps1", "rstd1", "seed1", "nt1", "shift1"))
        st2 = sb("st2", [P, TT, 6])
        mv2 = sb("mv2", [P, TT, 2])
        veps2, rstd2, seed2, nt2, shift2 = (sb(n, [P, TT]) for n in ("veps2", "rstd2", "seed2", "nt2", "shift2"))
        eps_sb = sb("eps_sb", [P, 1])
        rows1 = [sb(f"rows1_{i}", [P, TT, RW]) for i in range(2)]
        rows2 = [sb(f"rows2_{i}", [P, TT, RW]) for i in range(2)]
        padrows = sb("padrows", [P, RW])
        x2nT = sb("x2nT", [P, TT * P])
        lgx = sb("lgx", [P, TT, E1 + 2])
        lex = sb("lex", [P, TT, E1 + 2])
        top = sb("top", [P, TT, 8])
        topi = sb("topi", [P, TT, 8], U32)
        lsum = sb("lsum", [P, TT, 1])
        oh = [sb(f"oh{i}", [P, TT, 2, E1]) for i in range(2)]
        prod = sb("prod", [P, TT, 2, E1])
        chosen = sb("chosen", [P, TT, E1], BF16)
        nextrow = sb("nextrow", [P, E1])
        rk_sb = sb("rk_sb", [P, TT + 2, E1])
        lg_sb = sb("lg_sb", [P, TT, E1])
        rank = sb("rank", [P, TT, E1])
        slot = [sb(f"slot{i}", [P, TT, 2], U32) for i in range(2)]
        g8 = sb("g8", [P, TT, 2])
        part8 = sb("part8", [P, TT, D])
        iota9i, iota9 = sb("iota9i", [P, E1], I32), sb("iota9", [P, E1])
        ebasei, ebase = sb("ebasei", [P, E1], I32), sb("ebase", [P, E1])
        dest = sb("dest", [P, NT * 2], I32)
        cnt = sb("cnt", [P, E1])
        thr_i, thr = sb("thr_i", [P, MAXT], I32), sb("thr", [P, MAXT])
        tcmp = sb("tcmp", [P, E, MAXT])
        ntile, ntsum, gap = sb("ntile", [P, E]), sb("ntsum", [P, E]), sb("gap", [P, E])
        zero8 = sb("zero8", [P, E])
        jot_i, jot = sb("jot_i", [P, NJ], I32), sb("jot", [P, NJ])
        jcmp, jprod = sb("jcmp", [P, NJ, E]), sb("jprod", [P, NJ, E])
        jexp, jrow = sb("jexp", [P, NJ]), sb("jrow", [P, NJ])
        tab_w = sb("tab_w", [P, NJ], I32)
        tab_row = sb("tab_row", [P, NJ], I32)
        tab_pad = sb("tab_pad", [P, E], I32)
        zeros = sb("zeros", [P, 1024])
        R = 8
        xg = sb("xg", [P, R, RW])
        xgT = sb("xgT", [P, 2, P])
        w1_now = sb("w1_now", [P, 2, F])
        hT = sb("hT", [P, 2, F])
        yg = sb("yg", [P, 4, D])
        pair_sb = sb("pair_sb", [P, NT, 2 * D])
        out_sb = sb("out_sb", [P, NT, D])

        def psum(name, shape):
            return es.enter_context(nc.psum_tensor(name, shape, F32))

        ps_s = psum("ps_s", [P, G, 512])
        ps_t = [psum(f"ps_t{i}", [P, 512]) for i in range(2)]
        ps_av = psum("ps_av", [P, 512])
        ps_o = psum("ps_o", [P, 512])
        AV = ps_av[:, 0:H * (DH + 1)].rearrange("p (h d) -> p h d", d=DH + 1)
        ps_h = [ps_s[:, 0, :], ps_s[:, 1, :]]
        ps_xt, ps_y = [t[:, 0:P] for t in ps_t], [ps_av[:, 0:D], ps_o[:, 0:D]]

        ld_x = [sem(f"ld_x{b}") for b in range(B)]
        ld_ctx, ld_wk, ld_w, ld_ffn = sem("ld_ctx"), sem("ld_wk"), sem("ld_w"), sem("ld_ffn")
        ld_mask, ld_bq, ld_small = sem("ld_mask"), sem("ld_bq"), sem("ld_small")
        zero_ready, pads_ready = sem("zero_ready"), sem("pads_ready")
        pre_done = sem("pre_done")
        consts = sem("consts")
        pool_c, dve_c, act_c = sem("pool_c"), sem("dve_c"), sem("act_c")
        bqs_ready = sem("bqs_ready")
        lone_waits = {e.engine: sem(f"lone_waits_{n}") for n, e in (("dve", nc.vector), ("pool", nc.gpsimd))}
        xn_ready, xb_ready = sem("xn_ready"), sem("xb_ready")
        k_full, kT_ready = sem("k_full"), sem("kT_ready")
        v_full, v_ready = sem("v_full"), sem("v_ready")
        vbd_full, vbd_ready = sem("vbd_full"), sem("vbd_ready")
        kbd_ready = sem("kbd_ready")
        t_full, t_used = sem("t_full"), sem("t_used")
        s_full, s_used = sem("s_full"), sem("s_used")
        ex_ready = sem("ex_ready")
        av_full, av_ready = sem("av_full"), sem("av_ready")
        at_full, at_used = sem("at_full"), sem("at_used")
        o_full, x2_ready = sem("o_full"), sem("x2_ready")
        row_ready, rowb_ready = sem("row_ready"), sem("rowb_ready")
        lgx_ready, lex_ready = sem("lgx_ready"), sem("lex_ready")
        chosen_ready = sem("chosen_ready")
        slot_ready = sem("slot_ready")
        sent = [sem(f"sent{t}") for t in range(TT)]
        tab_ready, zeroed = sem("tab_ready"), sem("zeroed")
        stats_ready, seed_ready = sem("stats_ready"), sem("seed_ready")
        stats1_ready, seed1_ready, shift1_ready = sem("stats1_ready"), sem("seed1_ready"), sem("shift1_ready")
        shift_ready = sem("shift_ready")
        g_c, base_ready = sem("g_c"), sem("base_ready")
        pads_done = sem("pads_done")
        dest_ready, row2_ready = sem("dest_ready"), sem("row2_ready")
        got = [sem(f"got{u}") for u in range(R)]
        xt_full, xt_used = sem("xt_full"), sem("xt_used")
        h_full, h_used = sem("h_full"), sem("h_used")
        w1_ready = sem("w1_ready")
        y_full, y_used = sem("y_full"), sem("y_used")
        put = [sem(f"put{u}") for u in range(4)]
        pair_in = [sem(f"pair_in{k}") for k in range(len(CHUNKS))]
        out_ready, stored = sem("out_ready"), sem("stored")

        block = es.enter_context(nc.Block())

        FILLS = {"T0": 0, "T1": 3, "xn": 6, "T2": 7, "x2n": 10, "lg": 12, "T3": 13, "q": 16, "rk": 17}
        EACH = 18
        LN2_FILLS = (10, 11, 12, 17)
        ORDER = {"mid": list(range(EACH))}
        ORDER["first"] = [k for k in range(EACH) if k not in (0, 1, 2) + LN2_FILLS]
        ORDER["last"] = [k for k in range(EACH) if k not in (6, 16)]
        FILLS.update({"x2n'": 20, "lg'": 21, "rk'": 22})
        ORDER["tail"] = [0, 1, 2] + list(LN2_FILLS) + [20, 21, 22]
        PRE_XN, PRE_Q, PRE_V = B, B + 1, B + 2
        FIRST_FILL = B + 3
        MID_FILL = FIRST_FILL + len(ORDER["first"])
        LAST_FILL = MID_FILL + EACH * (B - 2)
        TAIL_FILL = LAST_FILL + len(ORDER["last"])

        def fill(kind, n, k):
            start = {"first": FIRST_FILL, "mid": MID_FILL, "last": LAST_FILL, "tail": TAIL_FILL}[kind]
            at = ORDER[kind].index(k)
            number = start + at
            if kind == "mid":
                return (n - 1) * EACH + number, number % 2
            return number, number % 2

        def part(r):
            if isinstance(r, int) and r >= B - 1:
                return B - 1, range(TT - 1, TT) if r == B else range(TT - 1)
            return r, range(TT)

        def buf(r):
            return int(isinstance(r, int) and r >= B - 1)

        def x2n_fills(r):
            if isinstance(r, int) and r == B:
                return [(FILLS["x2n'"], [TT - 1])]
            _, tiles = part(r)
            return [(FILLS["x2n"] + h, list(tiles)[2 * h:2 * h + 2]) for h in range(2)]

        def router_fill(r, what):
            if not isinstance(r, int):
                return fill("mid", r + 1, FILLS[what])
            if r < B - 1:
                return fill("last", r + 1, FILLS[what])
            return fill("tail", B, FILLS[what + "'" if r == B else what])

        def slots_of(r):
            _, tiles = part(r)
            return slice(tiles[0], tiles[-1] + 1), TT if isinstance(r, int) and r == B else 0

        def stand_alone(eng):
            eng.sem_inc(lone_waits[eng.engine], 1)

        def batches(eng, step):
            for t in range(TT):
                step("first", 0, t)
            with eng.Fori(1, B - 1) as n:
                for t in range(TT):
                    step("mid", n, t)
            for t in range(TT):
                step("last", B - 1, t)

        def write_pad(eng, e):
            row = eng.value_load(tab_pad[0:1, e:e + 1], min_val=0, max_val=DEAD - P)
            eng.dma_start(slots[bass.ds(row, P), :], padrows[:, :]).then_inc(pads_done, 16)

        @block.sync
        def _(sp):
            xv = x.rearrange("b (t p) d -> b p t d", p=P)
            x4 = x_sb[:, :].rearrange("p (b t d) -> p b t d", b=B, d=D)
            sp.dma_start(x4[:, 0], xv[0]).then_inc(ld_x[0], 16)
            sp.dma_start(ctx_sb[:, :, :], ctx_in.rearrange("b k d -> k b d")).then_inc(ld_ctx, 16)
            sp.dma_start(wk_sb[:, :], wk).then_inc(ld_wk, 16)
            for dst, src in ((wv_sb, wv), (wq_sb, wq)):
                sp.dma_start(dst[:, :], src).then_inc(ld_w, 16)
            for b in range(1, B):
                sp.dma_start(x4[:, b], xv[b]).then_inc(ld_x[b], 16)
            for dst, src in ((bo_sb, bo), (rb_sb, rb)):
                sp.dma_start(dst[:, :], src.partition_broadcast(P)).then_inc(ld_small, 16)
            sp.dma_start(wo_sb[:, :], wo).then_inc(ld_small, 16)
            sp.wait_ge(zeroed, 1)
            sp.dma_start(wr_sb[:, 0:E1], wr).then_inc(ld_small, 16)
            sp.wait_ge(zero_ready, 1)
            pz = pairs.rearrange("(p r) d -> p (r d)", p=P)
            for i in range(pz.shape[1] // 1024):
                sp.dma_start(pz[:, i * 1024:(i + 1) * 1024], zeros[:, :]).then_inc(pre_done, 16)
            sp.wait_ge(pads_ready, 2)
            sp.dma_start(slots[DEAD:DEAD + P, :], padrows[:, :]).then_inc(pre_done, 16)
            sp.dma_start(w1_sb[:, :].rearrange("p (e f) -> p e f", e=E),
                         w1.rearrange("e d f -> d e f")).then_inc(ld_ffn, 16)
            sp.dma_start(w2_sb[:, :].rearrange("p (e c d) -> p e c d", e=E, c=FC),
                         w2.rearrange("e (c p) d -> p e c d", p=P)).then_inc(ld_ffn, 16)
            sp.wait_ge(tab_ready, 1)
            for e in range(E // 2):
                write_pad(sp, e)
            sp.wait_ge(tab_ready, 2)
            sp.wait_ge(pads_done, 16 * E)
            sp.wait_ge(pre_done, 16 * (NTOK * TOPK // 1024 + 1))
            for t in range(TT):
                sp.wait_ge(sent[t], 32 * B)

            def load(j, u, first):
                if not first:
                    sp.wait_ge(put[u % 4], (j - R) * 4 + 16 - 4 * (u % 4))
                row = sp.value_load(tab_row[0:1, bass.ds(j, 1)], min_val=0, max_val=DEAD)
                sp.dma_start(xg[:, u, :], slots[bass.ds(row, P), :]).then_inc(got[u], 16)

            for u in range(R):
                load(u, u, True)
            with sp.Fori(1, NJ // R) as it:
                for u in range(R):
                    load(it * R + u, u, False)
            for u in range(4):
                sp.wait_ge(put[u], 16 * (NJ // 4))
            pv = pairs.rearrange("(t p c) d -> p t (c d)", p=P, c=2)
            for k, (a, z) in enumerate(CHUNKS):
                sp.dma_start(pair_sb[:, a:z, :], pv[:, a:z, :]).then_inc(pair_in[k], 16)
            ov = out.rearrange("b (t p) d -> p (b t) d", p=P)
            for k, (a, z) in enumerate(CHUNKS):
                sp.wait_ge(out_ready, k + 1)
                sp.dma_start(ov[:, a:z, :], out_sb[:, a:z, :]).then_inc(stored, 16)
            sp.wait_ge(stored, 16 * len(CHUNKS))

        @block.gpsimd
        def _(pool):
            chain = Tally(pool, pool_c)
            pool.memset(wr_sb[:, :], 0.0).then_inc(zeroed, 1)
            chain.link(pool.memset(ident[:, :], 0.0))
            pool.affine_select(out=ident[:, :], in_=ident[:, :], compare_op=ALU.not_equal, fill=1.0,
                               base=0, pattern=[[-1, P]], channel_multiplier=1).then_inc(consts, 1)
            chain.link(pool.memset(hm16[:, :], 1.0))
            chain.link(pool.affine_select(out=hm16[:, :], in_=hm16[:, :], compare_op=ALU.is_ge, fill=0.0,
                                          base=0, pattern=[[-DH, H]], channel_multiplier=1))
            pool.affine_select(out=hm16[:, :], in_=hm16[:, :], compare_op=ALU.is_ge, fill=0.0,
                               base=DH - 1, pattern=[[DH, H]], channel_multiplier=-1).then_inc(consts, 1)
            pool.memset(repeat[:, HK:HKP], 0.0).then_inc(consts, 1)
            pool.wait_ge(consts, 1)
            pool.tensor_copy(repeat[:, 0:HK].rearrange("p (h k) -> p h k", k=NK),
                             ident[0:NK, 0:NK].unsqueeze(1).to_broadcast([NK, H, NK])).then_inc(consts, 1)
            chain.link(pool.memset(headrow[:, :, :], 1.0))
            chain.link(pool.affine_select(out=headrow[:, :, :], in_=headrow[:, :, :], compare_op=ALU.is_ge,
                                          fill=0.0, base=0, pattern=[[P, NCH], [-NK, H]],
                                          channel_multiplier=1))
            pool.affine_select(out=headrow[:, :, :], in_=headrow[:, :, :], compare_op=ALU.is_ge, fill=0.0,
                               base=NK - 1, pattern=[[-P, NCH], [NK, H]],
                               channel_multiplier=-1).then_inc(consts, 1)
            pool.wait_ge(consts, 5)
            for c in range(NCH):
                i = pool.tensor_copy(headrow3[:, c, :, :], headrow[:, c, head0[c]:head0[c] + NH3].unsqueeze(2)
                                     .to_broadcast([P, NH3, DH + 1]))
            i.then_inc(consts, 1)
            pool.memset(ones_b[:, :], 1.0).then_inc(consts, 1)
            chain.link(pool.memset(upper_b[:, :], 1.0))
            pool.affine_select(out=upper_b[:, :], in_=upper_b[:, :], compare_op=ALU.is_gt, fill=0.0,
                               base=0, pattern=[[1, P]], channel_multiplier=-1).then_inc(consts, 1)
            pool.memset(ex[:, :, HK:HKP], 0.0).then_inc(consts, 1)
            pool.iota(iota9i[:, :], [[1, E1]], base=0, channel_multiplier=0).then_inc(consts, 1)
            pool.iota(ebasei[:, :], [[REGION, E1]], base=0, channel_multiplier=0).then_inc(consts, 1)
            pool.iota(dest[:, :], [[2 * P, NT], [1, 2]], base=0, channel_multiplier=2).then_inc(consts, 1)
            pool.iota(thr_i[:, :], [[P, MAXT]], base=0, channel_multiplier=0).then_inc(consts, 1)
            pool.iota(jot_i[:, :], [[1, NJ]], base=0, channel_multiplier=0).then_inc(consts, 1)
            def stage_k(n, first=False):
                if not first:
                    pool.wait_ge(s_full, n * 2 * TT)
                k = kT[:, bass.ds(n * NK, NK)].unsqueeze(1).to_broadcast([P, HG, NK])
                pool.tensor_tensor(kbd[:, :, :], k, hm4[:, :].unsqueeze(2).to_broadcast([P, HG, NK]),
                                   ALU.mult).then_inc(kbd_ready, 1)

            pool.wait_ge(kT_ready, 2)
            stage_k(0, first=True)
            pool.memset(vbd[:, :, :, NH3 * (DH + 1):VC], 0.0).then_inc(consts, 1)
            pool.memset(zeros[:, :], 0.0).then_inc(zero_ready, 1)
            pool.memset(padrows[:, 0:D + 1], 0.0).then_inc(pads_ready, 1)

            def xb(b):
                v = x_sb[:, b * TT * D:(b + 1) * TT * D].rearrange("p (t d) -> p t d", d=D)
                o = xb_sb[:, b * TT * D:(b + 1) * TT * D].rearrange("p (t d) -> p t d", d=D)
                pool.wait_ge(ld_x[b], 16)
                pool.tensor_tensor(o, v, bo_sb[:, :].unsqueeze(1).to_broadcast([P, TT, D]),
                                   ALU.add).then_inc(xb_ready, 1)

            def destinations(m, ready):
                to = dest[:, bass.ds(m * TT * 2, TT * 2)].rearrange("p (t c) -> p t c", c=2)
                for c, rows in enumerate((rows1[buf(m)], rows2[buf(m)])):
                    pool.tensor_copy(rows[:, :, D + 1:D + 2].bitcast(I32), to[:, :, c:c + 1]).then_inc(ready, 1)

            def prepare(m):
                pool.wait_ge(row_ready, m + 1)
                stand_alone(pool)
                pool.tensor_copy(rows2[0][:, :, 0:D], rows1[0][:, :, 0:D]).then_inc(rowb_ready, 1)
                destinations(m, rowb_ready)

            def send(r):
                k, tiles = buf(r), part(r)[1]
                if k:
                    pool.wait_ge(dest_ready, 2)
                    pool.wait_ge(row2_ready, r - B + 2)
                else:
                    pool.wait_ge(rowb_ready, (r + 1) * 3)
                    stand_alone(pool)
                pool.wait_ge(slot_ready, r + 1)
                stand_alone(pool)
                for t in tiles:
                    for c, rows in enumerate((rows1[k], rows2[k])):
                        pool.indirect_dma_start(
                            slots, bass.IndirectOffsetOnAxis(ap=slot[k][:, t, c:c + 1], axis=0),
                            rows[:, t, :], None, bounds_check=ROWS - 1,
                            oob_is_err=False).then_inc(sent[t], 16)

            def identity(m):
                k = buf(m)
                for c, rows in enumerate((rows1[k], rows2[k])):
                    pool.tensor_tensor(g8[:, :, c], oh[k][:, :, c, E], rows[:, :, D], ALU.mult).then_inc(g_c, 1)
                pool.wait_ge(g_c, m * 4 + 2)
                pool.tensor_tensor(g8[:, :, 0], g8[:, :, 0], g8[:, :, 1], ALU.add).then_inc(g_c, 1)
                pool.wait_ge(g_c, m * 4 + 3)
                pool.tensor_tensor(part8[:, :, :], rows1[k][:, :, 0:D], g8[:, :, 0:1].to_broadcast([P, TT, D]),
                                   ALU.mult).then_inc(g_c, 1)
                pool.wait_ge(g_c, m * 4 + 4)
                o = base_sb[:, bass.ds(m * TT * D, TT * D)].rearrange("p (t d) -> p t d", d=D)
                pool.tensor_tensor(o, o, part8[:, :, :], ALU.add).then_inc(base_ready, 1)

            pool.wait_ge(ld_small, 16 * 4)
            for b in range(B):
                xb(b)
            pool.wait_ge(consts, 14)
            destinations(B - 1, dest_ready)
            stage_k(1)
            with pool.Fori(1, B - 1) as n:
                stage_k(n + 1)
                prepare(n - 1)
                send(n - 1)
                identity(n - 1)
            prepare(B - 2)
            send(B - 2)
            send(B - 1)
            send(B)
            identity(B - 2)
            identity(B - 1)

            pool.wait_ge(pre_done, 16 * (NTOK * TOPK // 1024 + 1))

            def send_back(j, u):
                pool.wait_ge(y_used, j + 1)
                stand_alone(pool)
                pool.indirect_dma_start(
                    pairs, bass.IndirectOffsetOnAxis(ap=xg[:, u, D + 1:D + 2].bitcast(U32), axis=0),
                    yg[:, u % 4, :], None, bounds_check=NTOK * TOPK - 1,
                    oob_is_err=False).then_inc(put[u % 4], 16)

            with pool.Fori(0, NJ // R) as it:
                for u in range(R):
                    send_back(it * R + u, u)

        @block.scalar
        def _(act):
            act.preload_act_table_set("natural_log_exp_and_others")
            act.dma_start(bk_sb[:, :], bk.rearrange("(p o) -> p o", o=1)).then_inc(ld_mask, 16)
            act.dma_start(mask8[:, :], mask.rearrange("b k -> (b k)").partition_broadcast(P)).then_inc(ld_mask, 16)
            act.dma_start(bv_sb[:, :], bv.partition_broadcast(P)).then_inc(ld_mask, 16)
            act.dma_start(bq_sb[:, :], bq.rearrange("(p o) -> p o", o=1)).then_inc(ld_bq, 16)

            for b in range(B):
                act.wait_ge(t_full, b + 1)
                act.copy(ctxT[:, b, :], ps_t[b % 2][:, 0:NK]).then_inc(t_used, 1)

            def copy_fill(number, dst, src):
                act.wait_ge(t_full, number + 1)
                act.copy(dst, src).then_inc(t_used, 1)

            def store_q(number, bank):
                act.wait_ge(t_full, number + 1)
                act.activation(qT[:, :], ps_t[bank][:, :], ACT.Identity, bias=bqs_sb[:, 0:1],
                               scale=QSCALE).then_inc(t_used, 1)

            def seeds(seed, variance, count, ready):
                act.activation(seed, variance, ACT.Ln, bias=eps_sb[:, 0:1]).then_inc(act_c, 1)
                act.wait_ge(act_c, count)
                act.activation(seed, seed, ACT.Exp, scale=-0.5).then_inc(ready, 1)

            def store_xn(n):
                for t in range(TT):
                    at = n * TT + t
                    i = act.activation(xn_sb[:, D * t:D * (t + 1)], x_sb[:, bass.ds(at * D, D)], ACT.Identity,
                                       bias=shift1[:, bass.ds(at, 1)], scale=rstd1[:, bass.ds(at, 1)])
                i.then_inc(xn_ready, 1)

            def seeds2(r):
                act.wait_ge(stats_ready, r + 1)
                ts = slots_of(r)[0]
                seeds(seed2[:, ts], mv2[:, ts, 1], r + 3, seed_ready)

            def norm2_again(r):
                for t in part(r)[1]:
                    i = act.activation(rows2[1][:, t, 0:D], base_sb[:, ((B - 1) * TT + t) * D:((B - 1) * TT + t + 1) * D],
                                       ACT.Identity, bias=shift2[:, t:t + 1], scale=rstd2[:, t:t + 1])
                i.then_inc(row2_ready, 1)

            def norm2(r):
                m, tiles = part(r)
                act.wait_ge(shift_ready, r + 1)
                for t in tiles:
                    if not isinstance(r, int) or 0 < r < B - 1:
                        act.wait_ge(sent[t], m * 32)
                        if t == 0:
                            act.wait_ge(base_ready, m)
                            act.wait_ge(rowb_ready, m * 3)
                    i = act.activation(rows1[buf(r)][:, t, 0:D], base_sb[:, bass.ds((m * TT + t) * D, D)],
                                       ACT.Identity, bias=shift2[:, t:t + 1], scale=rstd2[:, t:t + 1])
                i.then_inc(row_ready, 1)

            act.wait_ge(stats1_ready, 1)
            seeds(seed1[:, 0:TT], mv1[:, 0:TT, 1], 1, seed1_ready)
            act.wait_ge(shift1_ready, 1)
            store_xn(0)
            copy_fill(PRE_XN, xnT[:, :], ps_t[PRE_XN % 2][:, :])
            act.wait_ge(ld_bq, 16)
            act.mul(bqs_sb[:, :], bq_sb[:, :], QSCALE).then_inc(bqs_ready, 1)
            act.wait_ge(bqs_ready, 1)
            store_q(PRE_Q, PRE_Q % 2)
            act.wait_ge(stats1_ready, B)
            seeds(seed1[:, TT:NT], mv1[:, TT:NT, 1], 2, seed1_ready)
            copy_fill(PRE_V, vtail[:, :], ps_t[PRE_V % 2][:, 0:2 * VB])

            def attn_t(i, par):
                act.wait_ge(at_full, i + 1)
                act.copy(avT[:, par, :], ps_o[:, 0:P]).then_inc(at_used, 1)

            def ex_t(kind, n, t, par):
                for p in range(3):
                    number, bank = fill(kind, n, FILLS[f"T{t}"] + p)
                    a, z = PIECES[p]
                    copy_fill(number, exT[:, par, P * a:P * z], ps_t[bank][:, 0:P * (z - a)])

            def x2n_t(r):
                for key, tiles in x2n_fills(r):
                    number, bank = (fill("tail", B, key) if isinstance(r, int) and r >= B - 1 else
                                    fill("last" if isinstance(r, int) else "mid", r + 1, key))
                    copy_fill(number, x2nT[:, P * tiles[0]:P * (tiles[-1] + 1)], ps_t[bank][:, 0:P * len(tiles)])

            def logits_out(r):
                number, bank = router_fill(r, "lg")
                ts, _ = slots_of(r)
                copy_fill(number, lg_sb[:, ts, :].rearrange("p t e -> p (t e)"),
                          ps_t[bank][:, 0:len(part(r)[1]) * E1])

            def router_exp(r):
                act.wait_ge(lgx_ready, r + 1)
                ts, _ = slots_of(r)
                act.activation(lex[:, ts, :], lgx[:, ts, :], ACT.Exp).then_inc(lex_ready, 1)

            def ranks_out(r):
                number, bank = router_fill(r, "rk")
                w, at = len(part(r)[1]) + 1, slots_of(r)[1]
                copy_fill(number, rk_sb[:, at:at + w, :].rearrange("p t e -> p (t e)"), ps_t[bank][:, 0:w * E1])

            def step(kind, n, t):
                i = n * TT + t
                if t == 2 and kind != "last":
                    number, bank = fill(kind, n, FILLS["xn"])
                    copy_fill(number, xnT[:, :], ps_t[bank][:, :])
                if t == 3 and kind != "first":
                    logits_out(n - 1)
                if kind != "first" or t >= 2:
                    attn_t(i - 2, t % 2)
                if kind != "first" or t >= 1:
                    ex_t(kind, n, t, (t + 1) % 2)
                if t == 1 and kind != "first":
                    seeds2(n - 1)
                if t == 2 and kind != "first":
                    norm2(n - 1)
                    x2n_t(n - 1)
                if t == 3 and kind != "last":
                    store_q(*fill(kind, n, FILLS["q"]))
                if t == 3 and kind == "mid":
                    router_exp(n - 1)
                    ranks_out(n - 1)
                act.wait_ge(s_used, i * 2 + 2)
                act.activation(ex[:, t % 2, 0:HK], sc[:, t % 2, :], ACT.Exp).then_inc(ex_ready, 1)
                if t == 3 and kind == "last":
                    router_exp(n - 1)
                    ranks_out(n - 1)
                if t == 0 and kind != "last":
                    if kind == "first":
                        act.wait_ge(shift1_ready, 2)
                    store_xn(n + 1)

            act.wait_ge(consts, 9)
            batches(act, step)
            attn_t(NT - 2, 0)
            ex_t("tail", B, 0, 1)
            seeds2(B - 1)
            norm2(B - 1)
            attn_t(NT - 1, 1)
            x2n_t(B - 1)
            norm2_again(B - 1)
            logits_out(B - 1)
            seeds2(B)
            router_exp(B - 1)
            ranks_out(B - 1)
            norm2(B)
            x2n_t(B)
            norm2_again(B)
            logits_out(B)
            router_exp(B)
            ranks_out(B)
            act.wait_ge(tab_ready, 1)
            for e in range(E // 2, E):
                write_pad(act, e)

            def gelu(j, u):
                act.wait_ge(h_full, j + 1)
                if not isinstance(j, int) or j >= 2:
                    act.wait_ge(y_full, j - 1)
                act.activation(hT[:, u % 2, :], ps_h[u % 2], ACT.Gelu).then_inc(h_used, 1)

            for u in range(R):
                gelu(u, u)
            with act.Fori(1, NJ // R) as it:
                for u in range(R):
                    gelu(it * R + u, u)

        @block.tensor
        def _(pe):
            def begin_fill(number):
                if not isinstance(number, int) or number >= 2:
                    pe.wait_ge(t_used, number - 1)

            pe.wait_ge(consts, 1)
            pe.wait_ge(ld_ctx, 16)
            for b in range(B):
                begin_fill(b)
                pe.transpose(ps_t[b % 2][:, 0:NK], ctx_sb[:, b, :], ident[0:NK, 0:NK]).then_inc(t_full, 1)
            pe.wait_ge(ld_wk, 16)
            pe.wait_ge(t_used, B)
            pe.matmul(ps_av[:, 0:B * NK], wk_sb[:, :], ctxT[:, :, :].rearrange("p b k -> p (b k)"), start=True,
                      stop=True).then_inc(k_full, 1)
            pe.wait_ge(ld_w, 32)
            for b in range(B):
                i = pe.matmul(ps_o[0:NK, D * b:D * (b + 1)], ctxT[:, b, :], wv_sb[:, :], start=True, stop=True)
            i.then_inc(v_full, 1)

            def fill_xn(number, bank, batch1):
                begin_fill(number)
                pe.wait_ge(xn_ready, batch1)
                for t in range(TT):
                    i = pe.transpose(ps_t[bank][:, P * t:P * (t + 1)], xn_sb[:, D * t:D * (t + 1)], ident[:, :])
                i.then_inc(t_full, 1)

            def fill_q(number, bank, xn_number):
                begin_fill(number)
                pe.wait_ge(t_used, xn_number + 1)
                pe.matmul(ps_t[bank][:, :], wq_sb[:, :], xnT[:, :], start=True, stop=True).then_inc(t_full, 1)

            fill_xn(PRE_XN, PRE_XN % 2, 1)
            fill_q(PRE_Q, PRE_Q % 2, PRE_XN)

            def expand_v():
                pe.wait_ge(consts, 4)
                pe.wait_ge(v_ready, 1)
                begin_fill(PRE_V)
                for c in range(NCH):
                    bank = (ps_av, ps_o, ps_t[PRE_V % 2])[c // 4]
                    i = pe.matmul(bank[:, VB * (c % 4):VB * (c % 4 + 1)], repeat[:, P * c:P * (c + 1)],
                                  v_sb[:, :, head0[c]:head0[c] + NH3, :].rearrange("k b h d -> k b (h d)"),
                                  start=True, stop=True)
                    if c in (3, 7):
                        i.then_inc(vbd_full, 1)
                i.then_inc(t_full, 1)

            def scores(kind, n, t):
                i = n * TT + t
                if t == 0:
                    if kind == "first":
                        pe.wait_ge(t_used, PRE_Q + 1)
                    else:
                        pe.wait_ge(t_used, Q_OF_0 + 1 + (n - 1) * EACH)
                    pe.wait_ge(kbd_ready, n + 1)
                for half in range(2):
                    if kind != "first" or t > 0:
                        pe.wait_ge(s_used, i * 2 - 1 + half)
                    for g in (2 * half, 2 * half + 1):
                        r = slice(32 * g, 32 * g + 32)
                        m = pe.matmul(ps_s[:, g, 0:GK], qT[r, P * t:P * (t + 1)],
                                      kbd[r, :, :].rearrange("p h k -> p (h k)"), start=True, stop=True)
                    m.then_inc(s_full, 1)

            def attn_t(i, par, first):
                pe.wait_ge(av_ready, i + 1)
                if not first:
                    pe.wait_ge(x2_ready, i)
                pe.transpose(ps_o[:, 0:P], av[:, par, :], ident[:, :]).then_inc(at_full, 1)

            def project(i, par):
                pe.wait_ge(at_used, i + 1)
                pe.matmul(ps_o[:, P:P + D], avT[:, par, :], wo_sb[:, :], start=True,
                          stop=True).then_inc(o_full, 1)

            def attend(kind, n, t, i, b, par, project_before=True, last_tile=False):
                def transposes(p):
                    number, bank = fill(kind, n, FILLS[f"T{t}"] + p)
                    begin_fill(number)
                    a, z = PIECES[p]
                    for c in range(a, z):
                        m = pe.transpose(ps_t[bank][:, P * (c - a):P * (c - a + 1)], ex[:, par, P * c:P * (c + 1)],
                                         ident[:, :])
                    m.then_inc(t_full, 1)

                def products(p):
                    number, _ = fill(kind, n, FILLS[f"T{t}"] + p)
                    pe.wait_ge(t_used, number + 1)
                    for c in range(*PIECES[p]):
                        v = vflat[:, bass.ds((b * NCH + c) * VC, VC)]
                        m = pe.matmul(ps_av[:, (DH + 1) * head0[c]:(DH + 1) * head0[c] + VC],
                                      exT[:, par, P * c:P * (c + 1)], v, start=c == 0, stop=c == NCH - 1,
                                      skip_group_check=True)
                    return m

                pe.wait_ge(ex_ready, i + 1)
                transposes(0)
                transposes(1)
                if project_before:
                    project(i - 1, (par + 1) % 2)
                transposes(2)
                if isinstance(i, int) and i == 0:
                    pe.wait_ge(vbd_ready, 3)
                else:
                    pe.wait_ge(av_ready, i)
                products(0)
                if last_tile and kind != "last":
                    number, bank = fill(kind, n, FILLS["q"])
                    fill_q(number, bank, fill(kind, n, FILLS["xn"])[0])
                products(1)
                if last_tile and kind == "mid":
                    ranks(n - 1)
                products(2).then_inc(av_full, 1)
                if last_tile and kind == "last":
                    ranks(n - 1)

            def fill_x2n(r):
                pe.wait_ge(row_ready, r + 1)
                for key, tiles in x2n_fills(r):
                    number, bank = (fill("tail", B, key) if isinstance(r, int) and r >= B - 1 else
                                    fill("last" if isinstance(r, int) else "mid", r + 1, key))
                    begin_fill(number)
                    for j, t in enumerate(tiles):
                        x_ = pe.transpose(ps_t[bank][:, P * j:P * (j + 1)], rows1[buf(r)][:, t, 0:D], ident[:, :])
                    x_.then_inc(t_full, 1)

            def logits(r):
                number, bank = router_fill(r, "lg")
                begin_fill(number)
                pe.wait_ge(t_used, number)
                for j, t in enumerate(part(r)[1]):
                    x_ = pe.matmul(ps_t[bank][:, E1 * j:E1 * j + WR], x2nT[:, P * t:P * (t + 1)], wr_sb[:, :],
                                   start=True, stop=True)
                x_.then_inc(t_full, 1)

            def ranks(r):
                number, bank = router_fill(r, "rk")
                rk, tiles = ps_t[bank], part(r)[1]
                w = len(tiles)
                begin_fill(number)
                pe.wait_ge(chosen_ready, r + 1)
                pe.matmul(rk[:, 0:E1], upper_b[:, :], chosen[:, tiles[0], :], start=True, stop=True)
                for j, t in enumerate(tiles):
                    i = pe.matmul(rk[:, E1 * (j + 1):E1 * (w + 1)], ones_b[:, :],
                                  chosen[:, t:t + 1, :].to_broadcast([P, w - j, E1]), start=j == 0,
                                  stop=w == 1, skip_group_check=True)
                if w > 1:
                    i = pe.matmul(rk[:, E1:E1 * w], upper_b[:, :],
                                  chosen[:, tiles[1]:tiles[-1] + 1, :].rearrange("p t e -> p (t e)"),
                                  start=False, stop=True, skip_group_check=True)
                i.then_inc(t_full, 1)

            vflat = vbd[:, :, :, :].rearrange("p b c v -> p (b c v)")
            Q_OF_0, _ = fill("first", 0, FILLS["q"])

            def step(kind, n, t):
                i = n * TT + t
                scores(kind, n, t)
                if t == 0 and kind == "first":
                    expand_v()
                if t == 3 and kind != "first":
                    logits(n - 1)
                if kind != "first" or t >= 2:
                    attn_t(i - 2, t % 2, kind == "first" and t == 2)
                if kind != "first" or t >= 1:
                    attend(kind, n, t, i - 1, n if t else n - 1, (t + 1) % 2, kind != "first" or t >= 2, t == 3)
                if t == 1 and kind != "last":
                    fill_xn(*fill(kind, n, FILLS["xn"]), n + 2)
                if t == 2 and kind != "first":
                    fill_x2n(n - 1)

            pe.wait_ge(kT_ready, 2)
            pe.wait_ge(ld_small, 16 * 4)
            batches(pe, step)
            attn_t(NT - 2, 0, False)
            attend("tail", B, 0, NT - 1, B - 1, 1)
            attn_t(NT - 1, 1, False)
            fill_x2n(B - 1)
            project(NT - 1, 1)
            for r in (B - 1, B):
                if r == B:
                    fill_x2n(r)
                logits(r)
                ranks(r)

            pe.wait_ge(tab_ready, 2)
            pe.wait_ge(ld_ffn, 32)

            def expert_of(j):
                return pe.value_load(tab_w[0:1, bass.ds(j, 1)], min_val=0, max_val=(E - 1) * F)

            def gather_t(j, u, it):
                pe.wait_ge(got[u], it * 16 + 16)
                if not isinstance(j, int) or j >= 2:
                    pe.wait_ge(xt_used, j - 1)
                pe.transpose(ps_xt[u % 2], xg[:, u, 0:D], ident[:, :]).then_inc(xt_full, 1)

            def up(j, par):
                pe.wait_ge(xt_used, j + 1)
                pe.wait_ge(w1_ready, j + 1)
                if not isinstance(j, int) or j >= 2:
                    pe.wait_ge(h_used, j - 1)
                for c in range(FC):
                    m = pe.matmul(ps_h[par][:, P * c:P * (c + 1)], w1_now[:, par, P * c:P * (c + 1)],
                                  xgT[:, par, :], start=True, stop=True)
                m.then_inc(h_full, 1)

            def down(j, par, e):
                pe.wait_ge(h_used, j + 1)
                if not isinstance(j, int) or j >= 2:
                    pe.wait_ge(y_used, j - 1)
                for c in range(FC):
                    m = pe.matmul(ps_y[par], hT[:, par, P * c:P * (c + 1)], w2_sb[:, bass.ds(e + P * c, D)],
                                  start=c == 0, stop=c == FC - 1)
                m.then_inc(y_full, 1)

            for j in range(NJ + 2):
                if j == R:
                    with pe.Fori(1, NJ // R) as it:
                        e = {-2: expert_of(it * R - 2)}
                        for u in range(R):
                            jj = it * R + u
                            gather_t(jj, u, it)
                            up(jj - 1, (u + 1) % 2)
                            if u < R - 1:
                                e[u - 1] = expert_of(jj - 1)
                            down(jj - 2, u % 2, e[u - 2])
                if R <= j < NJ:
                    continue
                if j < NJ:
                    gather_t(j, j, 0)
                if 0 <= j - 1 < NJ:
                    up(j - 1, (j - 1) % 2)
                if 0 <= j - 2 < NJ:
                    down(j - 2, j % 2, expert_of(j - 2))

        @block.vector
        def _(dve):
            chain = Tally(dve, dve_c)
            link = chain.link

            def stats1(n):
                dve.wait_ge(ld_x[n], 16)
                for t in range(n * TT, (n + 1) * TT):
                    i = dve.bn_stats(st1[:, t, :], x_sb[:, t * D:(t + 1) * D])
                link(i)
                for t in range(n * TT, (n + 1) * TT):
                    i = dve.bn_aggr(mv1[:, t, :], st1[:, t, :])
                i.then_inc(stats1_ready, 1)

            def refine(mv, veps, seed, nt, rstd, shift, tiles, seeded, count, ready):
                link(dve.tensor_scalar(veps[:, tiles], mv[:, tiles, 1], EPS, None, ALU.add))
                dve.wait_ge(seeded, count)
                link(dve.tensor_tensor(nt[:, tiles], seed[:, tiles], seed[:, tiles], ALU.mult))
                link(dve.scalar_tensor_tensor(nt[:, tiles], nt[:, tiles], -0.5, veps[:, tiles],
                                              ALU.mult, ALU.mult))
                link(dve.scalar_tensor_tensor(rstd[:, tiles], nt[:, tiles], 1.5, seed[:, tiles],
                                              ALU.add, ALU.mult))
                dve.scalar_tensor_tensor(shift[:, tiles], mv[:, tiles, 0], -1.0, rstd[:, tiles],
                                         ALU.mult, ALU.mult).then_inc(ready, 1)

            def refine1(tiles, count):
                dve.wait_ge(stats1_ready, 1 if count == 1 else B)
                refine(mv1, veps1, seed1, nt1, rstd1, shift1, tiles, seed1_ready, count, shift1_ready)

            def refine2(r):
                dve.wait_ge(stats_ready, r + 1)
                refine(mv2, veps2, seed2, nt2, rstd2, shift2, slots_of(r)[0], seed_ready, r + 1, shift_ready)

            chain.link(dve.memset(eps_sb[:, :], EPS))
            stats1(0)
            dve.wait_ge(consts, 2)
            dve.tensor_reduce(hm4[:, :], hm16[:, :].rearrange("p (g j) -> p j g", g=G), AX.X,
                              ALU.add).then_inc(kT_ready, 1)
            refine1(slice(0, TT), 1)
            dve.wait_ge(ld_mask, 16 * 3)
            dve.tensor_copy(maskf[:, :], mask8[:, :])
            link(dve.tensor_scalar(valid[:, :], mask8[:, :], -1.0, 1.0, ALU.mult, ALU.add))
            by_key = [P, B, NK]
            valid_b = valid[:, :].rearrange("p (b k) -> p b k", b=B)
            maskf_b = maskf[:, :].rearrange("p (b k) -> p b k", b=B)
            kT_b = kT[:, :].rearrange("p (b k) -> p b k", b=B)
            dve.tensor_tensor(valid_own[:, :, :], valid_b[0:NK], ident[0:NK, 0:NK].unsqueeze(1)
                              .to_broadcast([NK, B, NK]), ALU.mult)
            link(dve.tensor_reduce(nvalid[:, :], valid_b, AX.X, ALU.add))
            dve.tensor_reduce(validT[:, :], valid_own[:, :, :], AX.X, ALU.add)
            dve.reciprocal(nvalid[:, :], nvalid[:, :])
            dve.wait_ge(k_full, 1)
            link(dve.scalar_tensor_tensor(kT[:, :], ps_av[:, 0:B * NK], bk_sb[:, 0:1], valid[:, :],
                                          ALU.add, ALU.mult))
            link(dve.tensor_reduce(kmean[:, :], kT_b, AX.X, ALU.add))
            link(dve.tensor_tensor(kmean[:, :], kmean[:, :], nvalid[:, :], ALU.mult))
            link(dve.tensor_tensor(maskf_b, maskf_b, kmean[:, :].unsqueeze(2).to_broadcast(by_key), ALU.mult))
            dve.tensor_tensor(kT[:, :], kT[:, :], maskf[:, :], ALU.add).then_inc(kT_ready, 1)
            dve.wait_ge(v_full, 1)
            link(dve.tensor_tensor(v_sb[:, :, :, 0:DH], ps_o[0:NK, :].rearrange("k (b h d) -> k b h d", b=B, d=DH),
                                   bv_sb[0:NK, :].rearrange("k (h d) -> k h d", d=DH).unsqueeze(1)
                                   .to_broadcast([NK, B, H, DH]), ALU.add))
            dve.tensor_copy(v_sb[:, :, :, DH], validT[:, :].unsqueeze(2).to_broadcast([NK, B, H]))
            for b in range(B):
                i = dve.tensor_scalar(v_sb[:, b, :, 0:DH], v_sb[:, b, :, 0:DH], validT[:, b:b + 1], None, ALU.mult)
            i.then_inc(v_ready, 1)
            for b in range(1, B):
                stats1(b)
            dve.wait_ge(consts, 14)
            dve.wait_ge(ld_small, 16 * 4)
            dve.tensor_copy(iota9[:, :], iota9i[:, :])
            dve.memset(zero8[:, :], 0.0)
            dve.tensor_copy(thr[:, :], thr_i[:, :])
            dve.tensor_copy(jot[:, :], jot_i[:, :])
            dve.tensor_scalar(padrows[:, D + 1:D + 2].bitcast(I32), dest[:, 0:1], 0, NTOK * TOPK, ALU.mult,
                              ALU.add).then_inc(pads_ready, 1)
            link(dve.tensor_copy(ebase[:, :], ebasei[:, :]))
            link(dve.tensor_scalar(ebase[:, E:E1], ebase[:, E:E1], float(P), None, ALU.add))
            link(dve.tensor_copy(nextrow[:, :], ebase[:, :]))

            def less_max(kind, n, t):
                i = n * TT + t
                par = t % 2
                for half in range(2):
                    dve.wait_ge(s_full, i * 2 + half + 1)
                    s = ps_s[:, 2 * half:2 * half + 2, 0:GK].rearrange("p g (h k) -> p g h k", k=NK)
                    m = mx[:, par, 8 * half:8 * half + 8]
                    link(dve.tensor_reduce(m, s, AX.X, ALU.max))
                    if half == 0 and (kind != "first" or t >= 2):
                        dve.wait_ge(ex_ready, i - 1)
                    o = sc[:, par, 2 * GK * half:2 * GK * (half + 1)]
                    dve.tensor_tensor(o.rearrange("p (g h k) -> p g h k", g=2, k=NK), s,
                                      m.rearrange("p (g h) -> p g h", g=2).unsqueeze(3)
                                      .to_broadcast([P, 2, HG, NK]), ALU.subtract).then_inc(s_used, 1)

            def residual(i, t):
                dve.wait_ge(o_full, i + 1)
                o = base_sb[:, bass.ds(i * D, D)]
                x2 = dve.tensor_tensor(o, ps_o[:, P:P + D], xb_sb[:, bass.ds(i * D, D)], ALU.add)
                x2.then_inc(x2_ready, 1)
                dve.wait_ge(x2_ready, i + 1)
                stand_alone(dve)
                link(dve.bn_stats(st2[:, t, :], o))
                stand_alone(dve)
                return dve.bn_aggr(mv2[:, t, :], st2[:, t, :])

            def weigh(i, par):
                dve.wait_ge(av_full, i + 1)
                link(dve.reciprocal(rsum[:, :], AV[:, :, DH]))
                dve.tensor_tensor(av[:, par, :].rearrange("p (h d) -> p h d", d=DH), AV[:, :, 0:DH],
                                  rsum[:, :].unsqueeze(2).to_broadcast([P, H, DH]),
                                  ALU.mult).then_inc(av_ready, 1)

            def choose(r):
                ts, _ = slots_of(r)
                w = len(part(r)[1])
                one = oh[buf(r)]
                dve.wait_ge(t_used, router_fill(r, "lg")[0] + 1)
                link(dve.tensor_tensor(lgx[:, ts, 0:E1], lg_sb[:, ts, :],
                                       rb_sb[:, :].unsqueeze(1).to_broadcast([P, w, E1]), ALU.add))
                stand_alone(dve)
                for t in part(r)[1]:
                    i = dve.max(top[:, t, :], lgx[:, t, 0:E1])
                link(i)
                stand_alone(dve)
                for t in part(r)[1]:
                    i = dve.max_index(topi[:, t, :], top[:, t, :], lgx[:, t, 0:E1])
                dve.tensor_copy(lgx[:, ts, E1:E1 + 2], top[:, ts, 0:2])
                link(i)
                every = [P, w, 2, E1]
                link(dve.tensor_tensor(one[:, ts, :, :], iota9[:, :].unsqueeze(1).unsqueeze(1).to_broadcast(every),
                                       topi[:, ts, 0:2].unsqueeze(3).to_broadcast(every), ALU.is_equal))
                dve.tensor_tensor(chosen[:, ts, :], one[:, ts, 0, :], one[:, ts, 1, :], ALU.add).then_inc(chosen_ready, 1)
                dve.tensor_tensor(lgx[:, ts, :], lgx[:, ts, :], top[:, ts, 0:1].to_broadcast([P, w, E1 + 2]),
                                  ALU.subtract).then_inc(lgx_ready, 1)

            def place(r):
                k = buf(r)
                ts, at = slots_of(r)
                w = len(part(r)[1])
                dve.wait_ge(lex_ready, r + 1)
                link(dve.tensor_reduce(lsum[:, ts, :], lex[:, ts, 0:E1], AX.X, ALU.add))
                link(dve.reciprocal(lsum[:, ts, :], lsum[:, ts, :]))
                for c, rows in enumerate((rows1[k], rows2[k])):
                    dve.tensor_tensor(rows[:, ts, D:D + 1], lex[:, ts, E1 + c:E1 + c + 1], lsum[:, ts, :], ALU.mult)
                dve.wait_ge(t_used, router_fill(r, "rk")[0] + 1)
                link(dve.tensor_tensor(rank[:, ts, :], rk_sb[:, at:at + w, :],
                                       nextrow[:, :].unsqueeze(1).to_broadcast([P, w, E1]), ALU.add))
                dve.tensor_tensor(nextrow[:, :], nextrow[:, :], rk_sb[:, at + w, :], ALU.add)
                every = [P, w, 2, E1]
                link(dve.tensor_tensor(prod[:, ts, :, :], oh[k][:, ts, :, :],
                                       rank[:, ts, :].unsqueeze(2).to_broadcast(every), ALU.mult))
                with nc.allow_low_precision(reason="a slot is a whole number below 2^24"):
                    dve.tensor_reduce(slot[k][:, ts, :], prod[:, ts, :, :], AX.X, ALU.add).then_inc(slot_ready, 1)

            def spread_v():
                dve.wait_ge(consts, 15)
                for q, c in enumerate(range(0, NCH, 4)):
                    w = min(4, NCH - c)
                    if q < 2:
                        dve.wait_ge(vbd_full, q + 1)
                    else:
                        dve.wait_ge(t_used, PRE_V + 1)
                    dve.tensor_tensor(vbd[:, :, c:c + w, 0:NH3 * (DH + 1)],
                                      (ps_av, ps_o, vtail)[q][:, 0:w * VB].rearrange("p (c b v) -> p b c v", c=w, b=B),
                                      headrow3[:, c:c + w, :, :].rearrange("p c h d -> p c (h d)").unsqueeze(1)
                                      .to_broadcast([P, B, w, NH3 * (DH + 1)]), ALU.mult).then_inc(vbd_ready, 1)

            def step(kind, n, t):
                i = n * TT + t
                less_max(kind, n, t)
                if t == 0 and kind == "first":
                    refine1(slice(TT, NT), 2)
                    spread_v()
                if t == 2 and kind == "first":
                    dve.wait_ge(xb_ready, B)
                if t == 3 and kind != "first":
                    choose(n - 1)
                if kind != "first" or t >= 2:
                    i_ = residual(i - 2, (t + 2) % 4)
                    if t == 1:
                        i_.then_inc(stats_ready, 1)
                if kind != "first" or t >= 1:
                    weigh(i - 1, (t + 1) % 2)
                if t == 1 and kind != "first":
                    refine2(n - 1)
                if t == 3 and kind != "first":
                    place(n - 1)

            def steps():
                for t in range(TT):
                    step("first", 0, t)
                with dve.Fori(1, B - 1) as n:
                    chain.enter(n - 1, LINKS)
                    for t in range(TT):
                        step("mid", n, t)
                    chain.leave(B - 2)
                for t in range(TT):
                    step("last", B - 1, t)

            steps()
            residual(NT - 2, 2).then_inc(stats_ready, 1)
            refine2(B - 1)
            weigh(NT - 1, 1)
            residual(NT - 1, 3).then_inc(stats_ready, 1)
            choose(B - 1)
            refine2(B)
            place(B - 1)
            choose(B)
            place(B)

            dve.tensor_copy(tab_pad[:, :], nextrow[:, 0:E]).then_inc(tab_ready, 1)
            link(dve.tensor_tensor(cnt[:, :], nextrow[:, :], ebase[:, :], ALU.subtract))
            link(dve.tensor_tensor(tcmp[:, :, :], cnt[:, 0:E].unsqueeze(2).to_broadcast([P, E, MAXT]),
                                   thr[:, :].unsqueeze(1).to_broadcast([P, E, MAXT]), ALU.is_gt))
            link(dve.tensor_reduce(ntile[:, :], tcmp[:, :, :], AX.X, ALU.add))
            dve.tensor_scalar(gap[:, :], ntile[:, :], -float(P), float(REGION), ALU.mult, ALU.add)
            link(dve.tensor_tensor_scan(ntsum[:, :], ntile[:, :], zero8[:, :], 0.0, ALU.add, ALU.add))
            link(dve.tensor_tensor(jcmp[:, :, :], jot[:, :].unsqueeze(2).to_broadcast([P, NJ, E]),
                                   ntsum[:, :].unsqueeze(1).to_broadcast([P, NJ, E]), ALU.is_ge))
            dve.tensor_reduce(jexp[:, :], jcmp[:, :, :], AX.X, ALU.add)
            link(dve.tensor_tensor(jprod[:, :, :], jcmp[:, :, :], gap[:, :].unsqueeze(1).to_broadcast([P, NJ, E]),
                                   ALU.mult))
            link(dve.tensor_reduce(jrow[:, :], jprod[:, :, :], AX.X, ALU.add))
            dve.tensor_scalar(tab_w[:, :], jexp[:, :], float(E - 1), float(F), ALU.min, ALU.mult)
            link(dve.scalar_tensor_tensor(jrow[:, :], jot[:, :], float(P), jrow[:, :], ALU.mult, ALU.add))
            dve.tensor_scalar(tab_row[:, :], jrow[:, :], float(DEAD), None, ALU.min).then_inc(tab_ready, 1)

            def take_rows(j, par):
                dve.wait_ge(xt_full, j + 1)
                dve.tensor_copy(xgT[:, par, :], ps_xt[par]).then_inc(xt_used, 1)

            def take_w1(j, par):
                e = dve.value_load(tab_w[0:1, bass.ds(j, 1)], min_val=0, max_val=(E - 1) * F)
                if not isinstance(j, int) or j >= 2:
                    dve.wait_ge(h_full, j - 1)
                dve.tensor_copy(w1_now[:, par, :], w1_sb[:, bass.ds(e, F)]).then_inc(w1_ready, 1)

            def take_result(j, slot8, quads):
                dve.wait_ge(y_full, j + 1)
                if not (isinstance(quads, int) and quads == 0):
                    dve.wait_ge(put[slot8 % 4], quads * 16)
                dve.tensor_scalar(yg[:, slot8 % 4, :], ps_y[slot8 % 2], xg[:, slot8, D:D + 1], None,
                                  ALU.mult).then_inc(y_used, 1)

            dve.wait_ge(ld_ffn, 32)
            for j in range(NJ + 2):
                if j == R:
                    with dve.Fori(1, NJ // R) as it:
                        for u in range(R):
                            jj = it * R + u
                            take_w1(jj, u % 2)
                            take_rows(jj, u % 2)
                            quads = it * 2 + (u - 2) // 4
                            take_result(jj - 2, (u - 2) % 8, quads)
                if R <= j < NJ:
                    continue
                if j < NJ:
                    take_w1(j, j % 2)
                    take_rows(j, j % 2)
                if 0 <= j - 2 < NJ:
                    take_result(j - 2, (j - 2) % R, (j - 2) // 4)

            dve.wait_ge(base_ready, B)
            for k, (a, z) in enumerate(CHUNKS):
                dve.wait_ge(pair_in[k], 16)
                link(dve.tensor_tensor(out_sb[:, a:z, :], pair_sb[:, a:z, 0:D], pair_sb[:, a:z, D:2 * D], ALU.add))
                dve.tensor_tensor(out_sb[:, a:z, :], out_sb[:, a:z, :],
                                  base_sb[:, a * D:z * D].rearrange("p (t d) -> p t d", d=D),
                                  ALU.add).then_inc(out_ready, 1)


_INS = ["x", "ctx_1024", "mask_BxS2_bk0", "L0_xattn_Wq", "L0_xattn_bq", "L0_xattn_Wk", "L0_xattn_bk",
        "L0_xattn_Wv", "L0_xattn_bv", "L0_xattn_Wo", "L0_xattn_bo", "L0_ffn_router_w", "L0_ffn_router_b",
        "L0_ffn_w1", "L0_ffn_w2"]


def kernel(**inputs):
    import numpy as _np
    import concourse.bacc as _bacc
    from concourse import mybir as _mybir
    from concourse.bass_utils import run_bass_kernel_spmd as _run

    nc = _bacc.Bacc("TRN2", target_bir_lowering=False, num_devices=1)
    arrays, args = {}, []
    for name in _INS:
        a = _np.ascontiguousarray(inputs[name])
        arrays[f"in_{name}"] = a
        args.append(nc.dram_tensor(f"in_{name}", a.shape, _mybir.dt.from_np(a.dtype), kind="ExternalInput").ap())
    x = inputs["x"]
    tokens, width, experts = x.shape[0] * x.shape[1], x.shape[2], inputs["L0_ffn_w1"].shape[0]
    f32 = _mybir.dt.float32
    args.append(nc.dram_tensor("out", tuple(x.shape), f32, kind="ExternalOutput").ap())
    args.append(nc.dram_tensor("slots", (experts * (tokens + 128) + 128, width + 2), f32, kind="Internal").ap())
    args.append(nc.dram_tensor("pairs", (2 * tokens, width), f32, kind="Internal").ap())
    build(nc, *args)
    r = _run(nc, [arrays], core_ids=[0])
    return r.results[0]["out"]
```
